# Optimizing a Trainium2 kernel written in Bass

```python
import numpy as np
import jax
import jax.numpy as jnp

def _softmax(x, axis=-1):
    return jax.nn.softmax(x, axis=axis)

def _gelu(x):
    return jax.nn.gelu(x, approximate=True)

def _silu(x):
    return jax.nn.silu(x)

def _sigmoid(x):
    return jax.nn.sigmoid(x)

def _layernorm(x, axis=-1, eps=1e-05):
    m = jnp.mean(x, axis=axis, keepdims=True)
    v = jnp.var(x, axis=axis, keepdims=True)
    return (x - m) / jnp.sqrt(v + eps)

def _scatter_add(tgt, idx, src, axis=0):
    return tgt.at[idx].add(src)

def _segment_sum(src, seg, n):
    return jax.ops.segment_sum(src, seg, n)
kernel_name = 'mk_macaron_d1_jaxref_r4_bfeb35'

def setup_inputs(seed: int=0):
    np.random.seed(seed)
    _w = jnp.asarray

    def _L0_attn_setup():
        import jax, jax.numpy as jnp
        import numpy as np
        B, S, D = (4, 1024, 256)
        H = 16
        HD = D // H

        def feature_map(x):
            return jnp.exp(-jnp.square(x) * 0.5)
        key = jax.random.key(seed)
        ks = jax.random.split(key, 9)
        s = 1.0 / np.sqrt(D)
        return {'x': jax.random.normal(ks[0], (B, S, D), dtype=jnp.float32), 'Wq': jax.random.normal(ks[1], (D, D), dtype=jnp.float32) * s, 'bq': jax.random.normal(ks[2], (D,), dtype=jnp.float32) * s, 'Wk': jax.random.normal(ks[3], (D, D), dtype=jnp.float32) * s, 'bk': jax.random.normal(ks[4], (D,), dtype=jnp.float32) * s, 'Wv': jax.random.normal(ks[5], (D, D), dtype=jnp.float32) * s, 'bv': jax.random.normal(ks[6], (D,), dtype=jnp.float32) * s, 'Wo': jax.random.normal(ks[7], (D, D), dtype=jnp.float32) * s, 'bo': jax.random.normal(ks[8], (D,), dtype=jnp.float32) * s}
    _L0_attn_in = _L0_attn_setup()

    def _L0_ffn_setup():
        import jax, jax.numpy as jnp
        import numpy as np
        CAPACITY_FACTOR = 1.25
        key = jax.random.key(seed)
        k1, k2, k3, k4 = jax.random.split(key, 4)
        B, T, D, F, E = (4, 1024, 256, 1024, 8)
        s = 0.02
        return {'x': jax.random.normal(k1, (B, T, D), dtype=jnp.float32), 'wg': jax.random.normal(k2, (D, E), dtype=jnp.float32) * s, 'W1': jax.random.normal(k3, (E, D, F), dtype=jnp.float32) * s, 'b1': jnp.zeros((E, F), dtype=jnp.float32), 'W2': jax.random.normal(k4, (E, F, D), dtype=jnp.float32) * s, 'b2': jnp.zeros((E, D), dtype=jnp.float32)}
    _L0_ffn_in = _L0_ffn_setup()
    _d = {'L0_attn_x': _L0_attn_in['x'], 'L0_attn_Wq': _L0_attn_in['Wq'], 'L0_attn_bq': _L0_attn_in['bq'], 'L0_attn_Wk': _L0_attn_in['Wk'], 'L0_attn_bk': _L0_attn_in['bk'], 'L0_attn_Wv': _L0_attn_in['Wv'], 'L0_attn_bv': _L0_attn_in['bv'], 'L0_attn_Wo': _L0_attn_in['Wo'], 'L0_attn_bo': _L0_attn_in['bo'], 'L0_ffn_wg': _L0_ffn_in['wg'], 'L0_ffn_W1': _L0_ffn_in['W1'], 'L0_ffn_b1': _L0_ffn_in['b1'], 'L0_ffn_W2': _L0_ffn_in['W2'], 'L0_ffn_b2': _L0_ffn_in['b2']}
    _x0 = _d['L0_attn_x']
    _d['L0_attn_x'] = jax.random.normal(jax.random.fold_in(jax.random.key(seed), 1), (8, 512, 256), dtype=_x0.dtype)
    del _x0
    return _d

def reference(L0_attn_x, L0_attn_Wq, L0_attn_bq, L0_attn_Wk, L0_attn_bk, L0_attn_Wv, L0_attn_bv, L0_attn_Wo, L0_attn_bo, L0_ffn_wg, L0_ffn_W1, L0_ffn_b1, L0_ffn_W2, L0_ffn_b2):

    def _L0_attn_ref(x, Wq, bq, Wk, bk, Wv, bv, Wo, bo):
        import jax, jax.numpy as jnp
        import numpy as np
        B, S, D = (4, 1024, 256)
        H = 16
        HD = D // H

        def feature_map(x):
            return jnp.exp(-jnp.square(x) * 0.5)
        b, s, _ = x.shape
        q = feature_map((x @ Wq + bq).reshape(b, s, H, HD))
        k = feature_map((x @ Wk + bk).reshape(b, s, H, HD))
        v = (x @ Wv + bv).reshape(b, s, H, HD)
        coeff = jnp.sum(q * k, axis=-1, keepdims=True)
        qkv = coeff * v
        out = qkv.reshape(b, s, H * HD)
        return out @ Wo + bo

    def _L0_ffn_ref(x, wg, W1, b1, W2, b2):
        import jax, jax.numpy as jnp
        import numpy as np
        CAPACITY_FACTOR = 1.25
        B, T, D = x.shape
        E = wg.shape[1]
        N = B * T
        capacity = int(N / E * CAPACITY_FACTOR) + 1
        xf = x.reshape(N, D)
        logits = xf @ wg
        scores = jax.nn.softmax(logits, axis=-1)
        top1 = jnp.argmax(scores, axis=-1)
        combine_w = jnp.take_along_axis(scores, top1[:, None], axis=1)[:, 0]
        oh = jax.nn.one_hot(top1, E, dtype=jnp.int32)
        rank = jnp.take_along_axis(jnp.cumsum(oh, axis=0), top1[:, None], axis=1)[:, 0] - 1
        valid = rank < capacity
        trash = E * capacity
        slot = jnp.where(valid, top1 * capacity + rank, trash)
        buf = jnp.zeros((E * capacity + 1, D), dtype=x.dtype).at[slot].set(xf)
        eb = buf[:E * capacity].reshape(E, capacity, D)
        h = jax.nn.gelu(jnp.einsum('ecd,edf->ecf', eb, W1) + b1[:, None, :], approximate=False)
        y = jnp.einsum('ecf,efd->ecd', h, W2) + b2[:, None, :]
        yf = y.reshape(E * capacity, D)
        gathered = yf[jnp.minimum(slot, E * capacity - 1)]
        out_flat = jnp.where(valid[:, None], gathered, 0.0) * combine_w[:, None]
        return out_flat.reshape(B, T, D)
    x = L0_attn_x
    x = x + 0.5 * _L0_ffn_ref(_layernorm(x, axis=-1), L0_ffn_wg, L0_ffn_W1, L0_ffn_b1, L0_ffn_W2, L0_ffn_b2)
    x = x + _L0_attn_ref(_layernorm(x, axis=-1), L0_attn_Wq, L0_attn_bq, L0_attn_Wk, L0_attn_bk, L0_attn_Wv, L0_attn_bv, L0_attn_Wo, L0_attn_bo)
    x = x + 0.5 * _L0_ffn_ref(_layernorm(x, axis=-1), L0_ffn_wg, L0_ffn_W1, L0_ffn_b1, L0_ffn_W2, L0_ffn_b2)
    return x

_drawn_inputs = setup_inputs


def setup_inputs(seed=0):
    import zlib

    import numpy as np

    out = dict(_drawn_inputs(seed))
    spreads = {'L0_ffn_b1': (0.0, 0.8), 'L0_ffn_b2': (0.0, 0.776)}
    factors = {'L0_attn_bq': 5.461,
     'L0_attn_bk': 5.699,
     'L0_attn_bo': 7.665,
     'L0_ffn_wg': 3.876,
     'L0_ffn_W1': 5.173,
     'L0_ffn_W2': 4.786}
    for name, (base, spread) in spreads.items():
        noise = np.random.default_rng([zlib.crc32(name.encode()), seed]).standard_normal(out[name].shape)
        drawn = base * np.exp(spread * noise) if base else spread * noise
        out[name] = jnp.asarray(drawn.astype(out[name].dtype))
    for name, factor in factors.items():
        out[name] = (out[name] * factor).astype(out[name].dtype)
    return out
```

```python
from contextlib import ExitStack

import concourse.bass as bass
from concourse import mybir

F32 = mybir.dt.float32
F32R = mybir.dt.float32r
I32 = mybir.dt.int32
U32 = mybir.dt.uint32
ALU = mybir.AluOpType
ACT = mybir.ActivationFunctionType
AX = mybir.AxisListType

P = 128
N, D, E, F = 4096, 256, 8, 1024
HD = 16
KD, FB = D // P, F // P
T = N // P
TC = 4
C = T // TC
CW = TC * P
CAP = int(N / E * 1.25) + 1
SL = CAP + CAP % 2
ST = -(-SL // P)
TAIL = SL - (ST - 1) * P
GA = 3
GROUPS = ((0, GA * P, 0, GA), (GA * P, SL, GA, ST))
HW = GROUPS[0][1]
MEAN, RSTD, WGT, TOK, ROW = D, D + 1, D + 2, D + 3, D + 4
EPS = 1e-5
FAR = 1.0e6
NH, NRO, NY = 3, 3, ST
HU = 2 * FB


def macaron(nc, x, w12, b1, b2, wa, bqkv, bo, wg, out):
    with ExitStack() as ctx:
        def sb(name, shape, dt=F32):
            return ctx.enter_context(nc.sbuf_tensor(name, shape, dt))

        def sem(name):
            return ctx.enter_context(nc.semaphore(name))

        slots = nc.dram_tensor("slots", (E * SL, ROW), F32, kind="Internal").ap()
        x1 = nc.dram_tensor("x1", (N, D), F32, kind="Internal").ap()
        bank = [ctx.enter_context(nc.psum_tensor(f"bank{i}", [P, 512], F32)) for i in range(8)]

        xe = sb("xe", [P, T, ROW])
        raw1, raw2 = sb("raw1", [P, KD * F]), sb("raw2", [P, FB * D])
        w1h, w1l = sb("w1h", [P, KD, F], F32R), sb("w1l", [P, KD, F], F32R)
        w2h, w2l = sb("w2h", [P, FB, D], F32R), sb("w2l", [P, FB, D], F32R)
        wah, wal = sb("wah", [P, KD, 4, D], F32R), sb("wal", [P, KD, 4, D], F32R)
        hi_part, lo_part = sb("hi_part", [P, FB * SL], F32R), sb("lo_part", [P, FB * SL], F32R)
        zth, ztl = sb("zth", [P, KD, SL], F32R), sb("ztl", [P, KD, SL], F32R)
        ident, before, ones = sb("ident", [P, P]), sb("before", [P, P]), sb("ones", [P, P])
        head_f = sb("head_f", [P, P])
        head = sb("head", [P, P], F32R)
        wgs = sb("wgs", [P, KD, E])
        b1s = sb("b1s", [P, E * FB])
        bqs = sb("bqs", [P, 3, KD])
        bos = sb("bos", [P, D])
        half = sb("half", [P, TC])
        first_code = sb("first_code", [P, E])
        code_i = sb("code_i", [P, E], I32)
        slot_base = sb("slot_base", [P, E])
        base_i = sb("base_i", [P, E], I32)
        slot_pos = sb("slot_pos", [P, ST])
        pos_i = sb("pos_i", [P, ST], I32)
        tok_i = sb("tok_i", [P, T], I32)
        gate = sb("gate", [P, E, T])
        zero_row = sb("zero_row", [P, ROW])
        stats = sb("stats", [P, 2, TC, 6])
        dlt = sb("dlt", [P, T, E])
        code = sb("code", [P, T, E])
        hot = sb("hot", [P, E, T])
        incl = sb("incl", [P, E, T])
        tmp = sb("tmp", [P, E, T])
        best = sb("best", [P, 4, T])
        off = sb("off", [P, 2, E])
        unused = sb("unused", [P, E, ST])
        slot_i = sb("slot_i", [P, T], U32)
        tok_idx = sb("tok_idx", [P, 2, ST], U32)

        arena = sb("arena", [P, 10240])
        room = [0]

        def cut(n, restart=False):
            if restart:
                room[0] = 0
            a = arena[:, room[0]:room[0] + n]
            room[0] += n
            assert room[0] <= 10240
            return a

        za = cut(2 * TC * D, True).rearrange("p (b t d) -> p b t d", b=2, t=TC)
        zr = cut(TC * D).rearrange("p (t d) -> p t d", t=TC)
        zrt = cut(KD * CW).rearrange("p (k n) -> p k n", k=KD)
        sqq = cut(KD * CW).rearrange("p (k n) -> p k n", k=KD)
        sqk = cut(KD * CW).rearrange("p (k n) -> p k n", k=KD)
        vb = cut(KD * CW).rearrange("p (k n) -> p k n", k=KD)
        ob = cut(KD * CW).rearrange("p (k n) -> p k n", k=KD)
        xs = cut(2 * ST * ROW, True).rearrange("p (b t c) -> p b t c", b=2, t=ST)
        hbuf = cut(NH * HW).rearrange("p (b n) -> p b n", b=NH)
        zs = cut(2 * D).rearrange("p (b d) -> p b d", b=2)
        b2s = cut(2 * D).rearrange("p (b d) -> p b d", b=2)
        ro = cut(NRO * D).rearrange("p (b d) -> p b d", b=NRO)
        xb = cut(2 * D).rearrange("p (b d) -> p b d", b=2)

        def cut_r(t, a, n):
            return t[:, a:a + n].rearrange("p (k n) -> p k n", k=KD)

        zh = [cut_r(hi_part, b * KD * CW, KD * CW) for b in range(2)]
        zl = [cut_r(lo_part, b * KD * CW, KD * CW) for b in range(2)]
        eh, el = cut_r(hi_part, 2 * KD * CW, KD * CW), cut_r(lo_part, 2 * KD * CW, KD * CW)
        oh, ol = cut_r(hi_part, 3 * KD * CW, KD * CW), cut_r(lo_part, 3 * KD * CW, KD * CW)
        hh = hi_part[:].rearrange("p (f n) -> p f n", f=FB)
        hl = lo_part[:].rearrange("p (f n) -> p f n", f=FB)
        logits = bank[7][:, 0:T * E].rearrange("p (t e) -> p t e", t=T)

        s_x = [sem(f"s_x{c}") for c in range(C)]
        s_small = sem("s_small")
        s_wa = sem("s_wa")
        s_shape = sem("s_shape")
        s_const = sem("s_const")
        s_conv = sem("s_conv")
        s_zero = sem("s_zero")
        s_init = sem("s_init")
        s_wah, s_wal = sem("s_wah"), sem("s_wal")
        r_st, r_ag, r_ve, r_rs, r_z = (sem(f"r_{n}") for n in ("st", "ag", "ve", "rs", "z"))
        a_st, a_ag, a_ve, a_rs, a_z = (sem(f"a_{n}") for n in ("st", "ag", "ve", "rs", "z"))
        r_t, r_tc, r_lg = sem("r_t"), sem("r_tc"), sem("r_lg")
        rt_v, rt_d, rt_e, rt_off, rt_pre, rt_idx, rt_used = (
            sem(f"rt_{n}") for n in ("v", "d", "e", "off", "pre", "idx", "used"))
        s_disp = sem("s_disp")
        a_t, a_zh, a_zl, a_bo = sem("a_t"), sem("a_zh"), sem("a_zl"), sem("a_bo")
        a_qkv, a_ev, a_pair, a_exp, a_eh, a_el = (
            sem(f"a_{n}") for n in ("qkv", "ev", "pair", "exp", "eh", "el"))
        a_cf, a_o, a_oh, a_ol, a_y, a_x2 = (sem(f"a_{n}") for n in ("cf", "o", "oh", "ol", "y", "x2"))
        s_x2st = sem("s_x2st")
        e_raw1, e_raw2 = sem("e_raw1"), sem("e_raw2")
        e_w1h, e_w1l, e_w2h, e_w2l = sem("e_w1h"), sem("e_w1l"), sem("e_w2h"), sem("e_w2l")
        e_xs, e_b2 = [sem("e_xs0"), sem("e_xs1")], [sem("e_b20"), sem("e_b21")]
        e_z, e_tz, e_zh, e_zl = (sem(f"e_{n}") for n in ("z", "tz", "zh", "zl"))
        e_l1, e_g, e_hh, e_hl = sem("e_l1"), sem("e_g"), sem("e_hh"), sem("e_hl")
        e_y, e_xb, e_ro, e_idx = sem("e_y"), sem("e_xb"), sem("e_ro"), sem("e_idx")
        e_out = [sem(f"e_out{i}") for i in range(NRO)]

        x_rows = x.rearrange("(p t) d -> p t d", p=P)
        x1_rows = x1.rearrange("(p t) d -> p t d", p=P)
        out_rows = out.rearrange("(p t) d -> p t d", p=P)

        def after(e, s, n):
            if n > 0:
                e.wait_ge(s, n)

        block = ctx.enter_context(nc.Block())

        @block.sync
        def _(sp):
            def tiles(c):
                return slice(TC * c, TC * c + TC)

            for c in range(C):
                sp.dma_start(xe[:, tiles(c), 0:D], x_rows[:, tiles(c)]).then_inc(s_x[c], 16)
                if c == 0:
                    for dst, src in ((wgs, wg), (b1s, b1), (bqs, bqkv)):
                        sp.dma_start(dst[:], src).then_inc(s_small, 16)
                    sp.dma_start(bos[:], bo.partition_broadcast(P)[:, 0, :]).then_inc(s_small, 16)
                    sp.dma_start(raw1[:], wa).then_inc(s_wa, 16)
            sp.wait_ge(s_const, 1)
            rows = E * SL // 48
            for h in range(1):
                sp.dma_start(slots.rearrange("(p a) c -> p a c", p=48),
                             zero_row[0:48, None, :].broadcast_to([48, rows, ROW])).then_inc(s_zero, 16)
            for c in range(C):
                sp.wait_ge(s_x[c], 16)
                sp.dma_start(x1_rows[:, tiles(c)], xe[:, tiles(c), 0:D]).then_inc(s_init, 16)

            def weights1(g):
                if g == 0:
                    sp.wait_ge(s_wal, 1)
                else:
                    sp.wait_ge(e_w1l, KD * g)
                sp.dma_start(raw1[:], w12[g % E, :, 0:KD * F]).then_inc(e_raw1, 16)

            def weights2(g):
                after(sp, e_w2l, FB * g)
                sp.dma_start(raw2[:], w12[g % E, :, KD * F:]).then_inc(e_raw2, 16)

            def rows_of(g):
                e, b = g % E, g % 2
                if e == 0:
                    sp.wait_ge(s_disp, 16 * T * (g // E + 1))
                if e >= 2:
                    sp.wait_ge(e_ro, NY * (g - 1))
                else:
                    sp.wait_ge(rt_used, g // E + 1)
                base = e * SL
                full = (ST - 1) * P
                sp.dma_start(xs[:, b, 0:ST - 1, :],
                             slots[base:base + full].rearrange("(j p) c -> p j c", p=P)).then_inc(e_xs[b], 16)
                sp.dma_start(xs[0:TAIL, b, ST - 1, :], slots[base + full:base + SL]).then_inc(e_xs[b], 16)
                sp.dma_start(b2s[:, b, :], b2[e:e + 1].partition_broadcast(P)[:, 0, :]).then_inc(e_b2[b], 16)

            for ffn in range(2):
                g0 = E * ffn
                if ffn == 0:
                    weights1(0)
                    weights2(0)
                rows_of(g0)
                rows_of(g0 + 1)
                for e in range(E):
                    g = g0 + e
                    if g + 1 < 2 * E:
                        weights1(g + 1)
                        weights2(g + 1)
                    if e + 2 < E:
                        rows_of(g + 2)
                if ffn == 0:
                    for i in range(NRO):
                        sp.wait_ge(e_out[i], 16 * (E * NY // NRO))
                    for c in range(C):
                        sp.dma_start(xe[:, tiles(c), 0:D], x1_rows[:, tiles(c)]).then_inc(s_x[c], 16)
                    for c in range(C):
                        sp.wait_ge(a_x2, 2 * (c + 1))
                        sp.dma_start(out_rows[:, tiles(c)], xe[:, tiles(c), 0:D]).then_inc(s_x2st, 16)
            for i in range(NRO):
                sp.wait_ge(e_out[i], 16 * (2 * E * NY // NRO))

        @block.gpsimd
        def _(pool):
            g_ = nc.gpsimd
            g_.memset(zero_row[:], 0.0).then_inc(s_const, 1)
            g_.memset(ident[:], 0.0)
            g_.memset(ones[:], 1.0)
            g_.memset(before[:], 1.0)
            g_.memset(head_f[:], 1.0)
            g_.memset(gate[:], 1.0)
            g_.memset(half[:], -0.5)
            g_.iota(tok_i[:], pattern=[[1, T]], base=0, channel_multiplier=T)
            g_.iota(pos_i[:], pattern=[[P, ST]], base=0, channel_multiplier=1)
            g_.iota(code_i[:], pattern=[[-1, E]], base=E, channel_multiplier=0)
            g_.iota(base_i[:], pattern=[[SL, E]], base=-1, channel_multiplier=0).then_inc(s_shape, 1)
            pool.wait_ge(s_shape, 1)
            g_.memset(gate[:, :, 0:1], 0.0)
            g_.affine_select(out=ident[:], in_=ident[:], compare_op=ALU.not_equal, fill=1.0, base=0,
                             pattern=[[-1, P]], channel_multiplier=1)
            g_.affine_select(out=before[:], in_=before[:], compare_op=ALU.is_gt, fill=0.0, base=0,
                             pattern=[[1, P]], channel_multiplier=-1)
            blk = head_f[:].rearrange("p (h d) -> p h d", d=HD)
            g_.affine_select(out=blk, in_=blk, compare_op=ALU.is_ge, fill=0.0, base=0,
                             pattern=[[-HD, P // HD], [0, HD]], channel_multiplier=1).then_inc(s_shape, 1)
            pool.wait_ge(s_shape, 2)
            g_.affine_select(out=blk, in_=blk, compare_op=ALU.is_ge, fill=0.0, base=HD - 1,
                             pattern=[[HD, P // HD], [0, HD]], channel_multiplier=-1).then_inc(s_const, 1)

            def rstd(ve, rs, c, n):
                pool.wait_ge(ve, n + 1)
                v = xe[:, TC * c:TC * c + TC, RSTD]
                g_.tensor_tensor(v, v, half[:], ALU.pow).then_inc(rs, 1)

            def dispatch(ffn):
                pool.wait_ge(rt_idx, ffn + 1)
                if ffn == 0:
                    pool.wait_ge(s_zero, 16)
                for t in range(T):
                    g_.indirect_dma_start(out=slots, out_offset=bass.IndirectOffsetOnAxis(ap=slot_i[:, t:t + 1], axis=0),
                                          in_=xe[:, t, :], in_offset=None, bounds_check=E * SL - 1,
                                          oob_is_err=False).then_inc(s_disp, 16)

            def results(ffn):
                dst = (x1, out)[ffn]
                pool.wait_ge((s_init, s_x2st)[ffn], 16 * C)
                for y in range(E * NY):
                    yy = ffn * E * NY + y
                    g, j = yy // NY, yy % NY
                    rows = P if j < ST - 1 else TAIL
                    pool.wait_ge(e_idx, 2 * (g + 1))
                    pool.wait_ge(e_ro, yy + 1)
                    g_.indirect_dma_start(out=dst, out_offset=bass.IndirectOffsetOnAxis(
                        ap=tok_idx[0:rows, g % 2, j:j + 1], axis=0), in_=ro[0:rows, yy % NRO, :], in_offset=None,
                        bounds_check=N - 1, oob_is_err=False).then_inc(e_out[yy % NRO], 16)

            for c in range(C):
                rstd(r_ve, r_rs, c, c)
            dispatch(0)
            results(0)

            def add_bo(c):
                pool.wait_ge(a_z, c + 1)
                for t in range(TC * c, TC * c + TC):
                    i = g_.tensor_tensor(xe[:, t, 0:D], xe[:, t, 0:D], bos[:], ALU.add)
                i.then_inc(a_bo, 1)

            for s in range(-2, C + 1):
                if 0 <= s + 1 < C:
                    add_bo(s + 1)
                if 0 <= s - 1 < C:
                    rstd(r_ve, r_rs, s - 1, C + s - 1)
                if 0 <= s + 2 < C:
                    rstd(a_ve, a_rs, s + 2, s + 2)
            dispatch(1)
            results(1)

        @block.scalar
        def _(act):
            s_ = nc.scalar

            def router_copy(c, ffn):
                n = C * ffn + c
                for k in range(KD):
                    act.wait_ge(r_t, KD * n + k + 1)
                    after(act, r_lg, n)
                    s_.copy(zrt[:, k, :], bank[k][:]).then_inc(r_tc, 1)

            def router_exp(ffn):
                act.wait_ge(rt_d, ffn + 1)
                s_.activation(dlt[:], dlt[:], ACT.Exp).then_inc(rt_e, 1)

            def expert(g):
                for gi, (c0, c1, t0, t1) in enumerate(GROUPS):
                    for f in range(FB):
                        u = HU * g + FB * gi + f
                        act.wait_ge(e_l1, u + 1)
                        after(act, e_hl, u + 1 - NH)
                        e = g % E
                        s_.activation(hbuf[:, u % NH, 0:c1 - c0], bank[2 + u % 4][:, 0:c1 - c0], ACT.Gelu,
                                      bias=b1s[:, e * FB + f:e * FB + f + 1]).then_inc(e_g, 1)

            def expert_zh(g):
                for gi, (c0, c1, t0, t1) in enumerate(GROUPS):
                    for k in range(KD):
                        n = (2 * g + gi) * KD + k
                        act.wait_ge(e_tz, ST * g + t1)
                        after(act, e_l1, HU * g)
                        s_.copy(zth[:, k, c0:c1], bank[k][:, 0:c1 - c0]).then_inc(e_zh, 1)

            def w1_hi(g):
                act.wait_ge(e_raw1, 16 * (g + 1))
                after(act, e_l1, HU * g)
                for k in range(KD):
                    s_.copy(w1h[:, k, :], raw1[:, k * F:(k + 1) * F]).then_inc(e_w1h, 1)

            act.wait_ge(s_wa, 16)
            s_.copy(wah[:].rearrange("p k m d -> p (k m d)"), raw1[:]).then_inc(s_wah, 1)
            act.wait_ge(s_small, 64)
            for c in range(C):
                router_copy(c, 0)
            w1_hi(0)
            router_exp(0)
            for ffn in range(2):
                g0 = E * ffn
                expert_zh(g0)
                for e in range(E):
                    expert(g0 + e)
                    if g0 + e + 1 < 2 * E:
                        w1_hi(g0 + e + 1)
                    if e + 1 < E:
                        expert_zh(g0 + e + 1)
                if ffn == 1:
                    break

                def z_hi(c):
                    for k in range(KD):
                        act.wait_ge(a_t, KD * c + k + 1)
                        after(act, a_qkv, 6 * (c - 1))
                        s_.copy(zh[c % 2][:, k, :], bank[k][:]).then_inc(a_zh, 1)

                def o_hi(c, m):
                    act.wait_ge(a_o, KD * c + m + 1)
                    after(act, a_y, 2 * c)
                    s_.copy(oh[:, m, :], ob[:, m, :]).then_inc(a_oh, 1)

                def squares(c, m):
                    for i, (sq, which) in enumerate(((sqq, 0), (sqk, 1))):
                        u = 6 * c + 2 * m + i
                        act.wait_ge(a_qkv, u + 1)
                        after(act, a_el, KD * (c - 1) + m + 1)
                        s_.activation(sq[:, m, :], bank[2 + u % 3][:], ACT.Square,
                                      bias=bqs[:, which, m:m + 1]).then_inc(a_ev, 1)

                def exp_hi(c, m):
                    act.wait_ge(a_pair, KD * c + m + 1)
                    s_.activation(sqq[:, m, :], sqq[:, m, :], ACT.Exp, scale=-0.5).then_inc(a_exp, 1)
                    act.wait_ge(a_exp, KD * c + m + 1)
                    after(act, a_cf, KD * c)
                    s_.copy(eh[:, m, :], sqq[:, m, :]).then_inc(a_eh, 1)

                def values(c):
                    for m in range(KD):
                        u = 6 * c + 4 + m
                        act.wait_ge(a_qkv, u + 1)
                        after(act, a_o, KD * c)
                        s_.activation(vb[:, m, :], bank[2 + u % 3][:], ACT.Identity,
                                      bias=bqs[:, 2, m:m + 1]).then_inc(a_ev, 1)

                for s in range(-1, C + 2):
                    now, prev = 0 <= s < C, 0 <= s - 1 < C
                    if 0 <= s + 1 < C:
                        z_hi(s + 1)
                    if prev:
                        o_hi(s - 1, 0)
                    if now:
                        squares(s, 0)
                    if prev:
                        o_hi(s - 1, 1)
                    if now:
                        squares(s, 1)
                        exp_hi(s, 0)
                        values(s)
                        exp_hi(s, 1)
                    if 0 <= s - 2 < C:
                        router_copy(s - 2, 1)
                router_exp(1)

        @block.vector
        def _(dve):
            v_ = nc.vector
            pieces = lambda a: a.rearrange("p k m d -> p (k m d)")

            def ln_stats(c, n, st, ag, ve, par):
                for i in range(TC):
                    v_.bn_stats(stats[:, par, i, :], xe[:, TC * c + i, 0:D]).then_inc(st, 1)
                for i in range(TC):
                    dve.wait_ge(st, TC * n + i + 1)
                    v_.bn_aggr(xe[:, TC * c + i, MEAN:RSTD + 1], stats[:, par, i, :]).then_inc(ag, 1)
                dve.wait_ge(ag, TC * (n + 1))
                v = xe[:, TC * c:TC * c + TC, RSTD]
                v_.tensor_scalar(v, v, EPS, None, ALU.add).then_inc(ve, 1)

            def ln_norm(c, n, rs, z, zdone):
                dve.wait_ge(rs, n + 1)
                for i in range(TC):
                    t = TC * c + i
                    q = v_.tensor_scalar(z[:, i, :], xe[:, t, 0:D], xe[:, t, MEAN:MEAN + 1],
                                         xe[:, t, RSTD:RSTD + 1], ALU.subtract, ALU.mult)
                q.then_inc(zdone, 1)

            def route(ffn):
                k = [13 * ffn]

                def link(i):
                    k[0] += 1
                    i.then_inc(rt_v, 1)
                    dve.wait_ge(rt_v, k[0])

                dve.wait_ge(r_lg, C * (ffn + 1))
                link(v_.tensor_reduce(best[:, 0, :], logits, AX.X, ALU.max))
                v_.tensor_tensor(dlt[:], logits, best[:, 0, :].unsqueeze(2).broadcast_to([P, T, E]),
                                 ALU.subtract).then_inc(rt_pre, 1)
                dve.wait_ge(rt_pre, 3 * ffn + 1)
                v_.scalar_tensor_tensor(out=code[:], in0=dlt[:], scalar=0.0,
                                        in1=first_code[:].unsqueeze(1).broadcast_to([P, T, E]),
                                        op0=ALU.is_ge, op1=ALU.mult).then_inc(rt_d, 1)
                dve.wait_ge(rt_d, ffn + 1)
                link(v_.tensor_reduce(best[:, 1, :], code[:], AX.X, ALU.max))
                link(v_.tensor_tensor(hot[:].rearrange("p e t -> p t e"), code[:],
                                      best[:, 1, :].unsqueeze(2).broadcast_to([P, T, E]), ALU.is_equal))
                link(v_.tensor_tensor_scan(incl[:].rearrange("p e t -> p (e t)"),
                                           gate[:].rearrange("p e t -> p (e t)"),
                                           hot[:].rearrange("p e t -> p (e t)"), 0.0, ALU.mult, ALU.add))
                v_.tensor_copy(off[:, 0, :], incl[:, :, T - 1]).then_inc(rt_pre, 1)
                dve.wait_ge(rt_e, ffn + 1)
                link(v_.tensor_reduce(best[:, 2, :], dlt[:], AX.X, ALU.add))
                link(v_.reciprocal(best[:, 3, :], best[:, 2, :]))
                v_.tensor_scalar(xe[:, :, WGT], best[:, 3, :], 0.5, None, ALU.mult)
                dve.wait_ge(rt_off, ffn + 1)
                link(v_.tensor_tensor(incl[:], incl[:], bank[6][:, 0:E].unsqueeze(2).broadcast_to([P, E, T]),
                                      ALU.add))
                v_.tensor_scalar(tmp[:], incl[:], float(CAP), None, ALU.is_gt).then_inc(rt_pre, 1)
                dve.wait_ge(rt_pre, 3 * ffn + 3)
                link(v_.tensor_tensor(incl[:], incl[:], slot_base[:].unsqueeze(2).broadcast_to([P, E, T]), ALU.add))
                return k, link

            def route_end(ffn, k, link):
                link(v_.scalar_tensor_tensor(out=incl[:], in0=tmp[:], scalar=FAR, in1=incl[:],
                                             op0=ALU.mult, op1=ALU.add))
                link(v_.tensor_tensor(tmp[:], incl[:], hot[:], ALU.mult))
                link(v_.tensor_reduce(best[:, 1, :], tmp[:].rearrange("p e t -> p t e"), AX.X, ALU.add))
                v_.tensor_copy(slot_i[:], best[:, 1, :]).then_inc(rt_idx, 1)
                link(v_.tensor_scalar(off[:, 1, :], bank[6][:, E:2 * E], float(CAP), None, ALU.min))
                link(v_.tensor_tensor(unused[:], slot_pos[:].unsqueeze(1).broadcast_to([P, E, ST]),
                                      off[:, 1, :].unsqueeze(2).broadcast_to([P, E, ST]), ALU.is_ge))
                v_.tensor_scalar(unused[:], unused[:], FAR, None, ALU.mult).then_inc(rt_used, 1)

            def split_w1(g):
                for k in range(KD):
                    dve.wait_ge(e_w1h, KD * g + k + 1)
                    v_.tensor_tensor(w1l[:, k, :], raw1[:, k * F:(k + 1) * F], w1h[:, k, :].bitcast(F32),
                                     ALU.subtract).then_inc(e_w1l, 1)

            def split_w2(g, f):
                n = FB * g + f
                dve.wait_ge(e_raw2, 16 * (g + 1))
                after(dve, e_y, NY * g)
                r = raw2[:, f * D:(f + 1) * D]
                v_.tensor_copy(w2h[:, f, :], r).then_inc(e_w2h, 1)
                dve.wait_ge(e_w2h, n + 1)
                v_.tensor_tensor(w2l[:, f, :], r, w2h[:, f, :].bitcast(F32), ALU.subtract).then_inc(e_w2l, 1)

            def slot_z(g):
                b, e = g % 2, g % E
                dve.wait_ge(e_xs[b], 32 * (g // 2 + 1))
                for gi, (c0, c1, t0, t1) in enumerate(GROUPS):
                    for j in range(t0, t1):
                        rows = P if j < ST - 1 else TAIL
                        n = ST * g + j
                        after(dve, e_tz, n - 1)
                        v_.tensor_scalar(zs[0:rows, n % 2, :], xs[0:rows, b, j, 0:D], xs[0:rows, b, j, MEAN:MEAN + 1],
                                         xs[0:rows, b, j, RSTD:RSTD + 1], ALU.subtract, ALU.mult).then_inc(e_z, 1)
                    for k in range(KD):
                        n = (2 * g + gi) * KD + k
                        dve.wait_ge(e_zh, n + 1)
                        v_.tensor_tensor(ztl[:, k, c0:c1], bank[k][:, 0:c1 - c0], zth[:, k, c0:c1].bitcast(F32),
                                         ALU.subtract).then_inc(e_zl, 1)
                after(dve, e_ro, NY * (g - 1))
                if g >= 2:
                    for i in range(NRO):
                        dve.wait_ge(e_out[i], 16 * NY // NRO * (g - 1))
                v_.tensor_tensor(tok_idx[:, b, 0:ST - 1], xs[:, b, 0:ST - 1, TOK], unused[:, e, 0:ST - 1],
                                 ALU.add).then_inc(e_idx, 1)
                v_.tensor_tensor(tok_idx[0:TAIL, b, ST - 1:ST], xs[0:TAIL, b, ST - 1, TOK:TOK + 1],
                                 unused[0:TAIL, e, ST - 1:ST], ALU.add).then_inc(e_idx, 1)

            def hidden(g):
                for gi, (c0, c1, t0, t1) in enumerate(GROUPS):
                    for f in range(FB):
                        u = HU * g + FB * gi + f
                        h = hbuf[:, u % NH, 0:c1 - c0]
                        dve.wait_ge(e_g, u + 1)
                        after(dve, e_y, NY * (g - 1) + t1)
                        v_.tensor_copy(hh[:, f, c0:c1], h).then_inc(e_hh, 1)
                        dve.wait_ge(e_hh, u + 1)
                        v_.tensor_tensor(hl[:, f, c0:c1], h, hh[:, f, c0:c1].bitcast(F32),
                                         ALU.subtract).then_inc(e_hl, 1)
                        if gi == 0:
                            split_w2(g, f)

            def result(g, j):
                b, yy = g % 2, NY * g + j
                rows = P if j < ST - 1 else TAIL
                w = xs[0:rows, b, j, WGT:WGT + 1]
                if j == 0:
                    dve.wait_ge(e_b2[b], 16 * (g // 2 + 1))
                v_.scalar_tensor_tensor(out=xb[0:rows, yy % 2, :], in0=b2s[0:rows, b, :], scalar=w,
                                        in1=xs[0:rows, b, j, 0:D], op0=ALU.mult, op1=ALU.add).then_inc(e_xb, 1)
                dve.wait_ge(e_xb, yy + 1)
                dve.wait_ge(e_y, yy + 1)
                after(dve, e_out[yy % NRO], 16 * (yy // NRO))
                v_.scalar_tensor_tensor(out=ro[0:rows, yy % NRO, :], in0=bank[6 + yy % 2][0:rows, 0:D], scalar=w,
                                        in1=xb[0:rows, yy % 2, :], op0=ALU.mult, op1=ALU.add).then_inc(e_ro, 1)

            dve.wait_ge(s_const, 2)
            v_.tensor_copy(head[:], head_f[:])
            v_.tensor_copy(xe[:, :, TOK], tok_i[:])
            v_.tensor_copy(slot_pos[:], pos_i[:])
            v_.tensor_copy(first_code[:], code_i[:])
            v_.tensor_copy(slot_base[:], base_i[:]).then_inc(s_conv, 1)
            for c in range(C):
                dve.wait_ge(s_x[c], 16)
                ln_stats(c, c, r_st, r_ag, r_ve, 0)
                after(dve, r_t, KD * c)
                ln_norm(c, c, r_rs, zr, r_z)
                if c == 1:
                    dve.wait_ge(s_wah, 1)
                    v_.tensor_tensor(pieces(wal[:]), raw1[:], pieces(wah[:]).bitcast(F32),
                                     ALU.subtract).then_inc(s_wal, 1)
            split_w1(0)
            for ffn in range(2):
                k, link = route(ffn)
                route_end(ffn, k, link)
                g0 = E * ffn
                slot_z(g0)
                for e in range(E):
                    g = g0 + e
                    hidden(g)
                    for j in range(3):
                        result(g, j)
                    if g + 1 < 2 * E:
                        split_w1(g + 1)
                    if e + 1 < E:
                        slot_z(g + 1)
                    for j in range(3, ST):
                        result(g, j)
                if ffn == 1:
                    break

                def z_lo(c):
                    for m in range(KD):
                        dve.wait_ge(a_zh, KD * c + m + 1)
                        v_.tensor_tensor(zl[c % 2][:, m, :], bank[m][:], zh[c % 2][:, m, :].bitcast(F32),
                                         ALU.subtract).then_inc(a_zl, 1)

                def weigh(c, m):
                    dve.wait_ge(a_cf, KD * c + m + 1)
                    dve.wait_ge(a_ev, 6 * c + 5 + m)
                    after(dve, a_ol, KD * (c - 1) + m + 1)
                    after(dve, a_oh, KD * (c - 1) + m + 1)
                    v_.tensor_tensor(ob[:, m, :], bank[5][:], vb[:, m, :], ALU.mult).then_inc(a_o, 1)

                def o_lo(c, m):
                    dve.wait_ge(a_oh, KD * c + m + 1)
                    v_.tensor_tensor(ol[:, m, :], ob[:, m, :], oh[:, m, :].bitcast(F32),
                                     ALU.subtract).then_inc(a_ol, 1)

                def pair(c, m):
                    dve.wait_ge(a_ev, 6 * c + 2 * m + 2)
                    v_.tensor_tensor(sqq[:, m, :], sqq[:, m, :], sqk[:, m, :], ALU.add).then_inc(a_pair, 1)

                def e_lo(c, m):
                    dve.wait_ge(a_eh, KD * c + m + 1)
                    v_.tensor_tensor(el[:, m, :], sqq[:, m, :], eh[:, m, :].bitcast(F32),
                                     ALU.subtract).then_inc(a_el, 1)

                def add_y(c):
                    dve.wait_ge(a_bo, c + 1)
                    for h in range(2 * c, 2 * c + 2):
                        dve.wait_ge(a_y, h + 1)
                        xt = xe[:, 2 * h:2 * h + 2, 0:D]
                        v_.tensor_tensor(xt, bank[6][:].rearrange("p (t d) -> p t d", t=2), xt,
                                         ALU.add).then_inc(a_x2, 1)

                for s in range(-2, C + 1):
                    now, prev = 0 <= s < C, 0 <= s - 1 < C
                    if 0 <= s + 1 < C:
                        z_lo(s + 1)
                    if prev:
                        weigh(s - 1, 0)
                        o_lo(s - 1, 0)
                    if now:
                        pair(s, 0)
                    if prev:
                        weigh(s - 1, 1)
                        o_lo(s - 1, 1)
                    if now:
                        pair(s, 1)
                        e_lo(s, 0)
                    if prev:
                        add_y(s - 1)
                    if now:
                        e_lo(s, 1)
                    if prev:
                        dve.wait_ge(a_x2, 2 * s)
                        ln_stats(s - 1, C + s - 1, r_st, r_ag, r_ve, 0)
                    if 0 <= s + 2 < C:
                        dve.wait_ge(s_x[s + 2], 32)
                        ln_stats(s + 2, s + 2, a_st, a_ag, a_ve, 1)
                    if prev:
                        after(dve, r_t, KD * (C + s - 1))
                        ln_norm(s - 1, C + s - 1, r_rs, zr, r_z)
                    if 0 <= s + 2 < C:
                        after(dve, a_t, KD * (s + 1))
                        ln_norm(s + 2, s + 2, a_rs, za[:, 0], a_z)

        @block.tensor
        def _(pe):
            t_ = nc.tensor

            def three(o, ah, al, bh, bl, first, last):
                t_.matmul(o, ah, bh, start=first, stop=False)
                t_.matmul(o, ah, bl, start=False, stop=False)
                return t_.matmul(o, al, bh, start=False, stop=last)

            def turn(c, n, z, zdone, done):
                pe.wait_ge(zdone, n + 1)
                for k in range(KD):
                    for i in range(TC):
                        q = t_.transpose(bank[k][:, i * P:(i + 1) * P], z[:, i, k * P:(k + 1) * P], ident[:])
                    q.then_inc(done, 1)

            def router_logits(c, ffn):
                n = C * ffn + c
                pe.wait_ge(r_tc, KD * (n + 1))
                for i in range(TC):
                    for k in range(KD):
                        q = t_.matmul(logits[:, TC * c + i, :], zrt[:, k, i * P:(i + 1) * P], wgs[:, k, :],
                                      start=(k == 0), stop=(k == KD - 1))
                q.then_inc(r_lg, 1)

            def counts(ffn):
                pe.wait_ge(rt_pre, 3 * ffn + 2)
                t_.matmul(bank[6][:, 0:E], before[:], off[:, 0, :], start=True, stop=True)
                t_.matmul(bank[6][:, E:2 * E], ones[:], off[:, 0, :], start=True, stop=True).then_inc(rt_off, 1)

            def slots_t(g, gi):
                c0, c1, t0, t1 = GROUPS[gi]
                m = 2 * g + gi
                after(pe, e_zl, KD * m)
                for j in range(t0, t1):
                    rows = P if j < ST - 1 else TAIL
                    n = ST * g + j
                    pe.wait_ge(e_z, n + 1)
                    for k in range(KD):
                        q = t_.transpose(bank[k][:, (j - t0) * P:(j - t0) * P + rows],
                                         zs[0:rows, n % 2, k * P:(k + 1) * P], ident[0:rows, 0:rows])
                    q.then_inc(e_tz, 1)

            def layer1(g, gi):
                c0, c1, t0, t1 = GROUPS[gi]
                pe.wait_ge(e_zl, KD * (2 * g + gi + 1))
                pe.wait_ge(e_w1l, KD * (g + 1))
                for f in range(FB):
                    u = HU * g + FB * gi + f
                    after(pe, e_g, u - 3)
                    o = bank[2 + u % 4][:, 0:c1 - c0]
                    for k in range(KD):
                        fs = slice(f * P, (f + 1) * P)
                        q = three(o, w1h[:, k, fs], w1l[:, k, fs], zth[:, k, c0:c1], ztl[:, k, c0:c1],
                                  k == 0, k == KD - 1)
                    q.then_inc(e_l1, 1)

            def layer2(g, j):
                gi = 0 if j < GA else 1
                yy = NY * g + j
                rows = P if j < ST - 1 else TAIL
                pe.wait_ge(e_hl, HU * g + FB * (gi + 1))
                pe.wait_ge(e_w2l, FB * (g + 1))
                after(pe, e_ro, yy - 1)
                o = bank[6 + yy % 2][0:rows, 0:D]
                for f in range(FB):
                    ns = slice(j * P, j * P + rows)
                    q = three(o, hh[:, f, ns], hl[:, f, ns], w2h[:, f, :], w2l[:, f, :], f == 0, f == FB - 1)
                q.then_inc(e_y, 1)

            pe.wait_ge(s_const, 2)
            pe.wait_ge(s_small, 64)
            pe.wait_ge(s_conv, 1)
            for c in range(C):
                after(pe, r_tc, KD * c)
                turn(c, c, zr, r_z, r_t)
                router_logits(c, 0)
            for ffn in range(2):
                counts(ffn)
                g0 = E * ffn
                slots_t(g0, 0)
                slots_t(g0, 1)
                for e in range(E):
                    g = g0 + e
                    layer1(g, 0)
                    layer1(g, 1)
                    for j in range(3):
                        layer2(g, j)
                    if e + 1 < E:
                        slots_t(g + 1, 0)
                        slots_t(g + 1, 1)
                    for j in range(3, ST):
                        layer2(g, j)
                if ffn == 1:
                    break

                def qkv(c, i):
                    which, m = ((0, 0), (1, 0), (0, 1), (1, 1), (2, 0), (2, 1))[i]
                    u = 6 * c + i
                    pe.wait_ge(a_zl, KD * (c + 1))
                    after(pe, a_ev, u - 2)
                    ms = slice(m * P, (m + 1) * P)
                    for k in range(KD):
                        q = three(bank[2 + u % 3][:], wah[:, k, which, ms], wal[:, k, which, ms],
                                  zh[c % 2][:, k, :], zl[c % 2][:, k, :], k == 0, k == KD - 1)
                    q.then_inc(a_qkv, 1)

                def coeff(c, m):
                    pe.wait_ge(a_el, KD * c + m + 1)
                    after(pe, a_o, KD * c + m)
                    t_.matmul(bank[5][:], head[:], eh[:, m, :], start=True, stop=False)
                    t_.matmul(bank[5][:], head[:], el[:, m, :], start=False, stop=True).then_inc(a_cf, 1)

                def project(c, h):
                    pe.wait_ge(a_ol, KD * (c + 1))
                    after(pe, a_x2, 2 * c + h)
                    for i in range(2 * h, 2 * h + 2):
                        for k in range(KD):
                            ns = slice(i * P, (i + 1) * P)
                            q = three(bank[6][:, (i % 2) * D:(i % 2) * D + D], oh[:, k, ns], ol[:, k, ns],
                                      wah[:, k, 3, :], wal[:, k, 3, :], k == 0, k == KD - 1)
                    q.then_inc(a_y, 1)

                for s in range(-1, C + 2):
                    now, prev = 0 <= s < C, 0 <= s - 1 < C
                    if 0 <= s + 1 < C:
                        after(pe, r_tc, KD * (C + s - 2))
                        turn(s + 1, s + 1, za[:, 0], a_z, a_t)
                    if prev:
                        coeff(s - 1, 0)
                    if now:
                        for i in range(3):
                            qkv(s, i)
                    if prev:
                        coeff(s - 1, 1)
                    if now:
                        for i in range(3, 6):
                            qkv(s, i)
                    if prev:
                        project(s - 1, 0)
                    if 0 <= s - 2 < C:
                        after(pe, a_zl, KD * min(s + 2, C))
                        turn(s - 2, C + s - 2, zr, r_z, r_t)
                    if prev:
                        project(s - 1, 1)
                    if 0 <= s - 2 < C:
                        router_logits(s - 2, 1)


_OUT = (8, 512, 256)


def kernel(L0_attn_x, L0_attn_Wq, L0_attn_bq, L0_attn_Wk, L0_attn_bk, L0_attn_Wv, L0_attn_bv, L0_attn_Wo,
           L0_attn_bo, L0_ffn_wg, L0_ffn_W1, L0_ffn_b1, L0_ffn_W2, L0_ffn_b2):
    import numpy as np
    import concourse.bacc as bacc
    from concourse.bass_utils import run_bass_kernel_spmd

    a = np.ascontiguousarray
    wa = np.stack([L0_attn_Wq, L0_attn_Wk, L0_attn_Wv, L0_attn_Wo], 1)
    w1 = np.asarray(L0_ffn_W1).reshape(E, KD, P, F).transpose(0, 2, 1, 3).reshape(E, P, KD * F)
    w2 = np.asarray(L0_ffn_W2).reshape(E, FB, P, D).transpose(0, 2, 1, 3).reshape(E, P, FB * D)
    arrays = {
        "x": a(np.asarray(L0_attn_x).reshape(N, D)),
        "w12": a(np.concatenate([w1, w2], 2)),
        "b1": a(np.asarray(L0_ffn_b1).reshape(E, FB, P).transpose(2, 0, 1).reshape(P, E * FB)),
        "b2": a(np.asarray(L0_ffn_b2)),
        "wa": a(wa.reshape(KD, P, 4 * D).transpose(1, 0, 2).reshape(P, KD * 4 * D)),
        "bqkv": a(np.stack([L0_attn_bq, L0_attn_bk, L0_attn_bv]).reshape(3, KD, P).transpose(2, 0, 1)),
        "bo": a(np.asarray(L0_attn_bo).reshape(1, D)),
        "wg": a(np.asarray(L0_ffn_wg).reshape(KD, P, E).transpose(1, 0, 2)),
    }
    nc = bacc.Bacc("TRN2", target_bir_lowering=False, num_devices=1)
    args = [nc.dram_tensor(n, v.shape, mybir.dt.from_np(v.dtype), kind="ExternalInput").ap()
            for n, v in arrays.items()]
    out = nc.dram_tensor("out", (N, D), F32, kind="ExternalOutput").ap()
    macaron(nc, *args, out)
    r = run_bass_kernel_spmd(nc, [arrays], core_ids=[0])
    return r.results[0]["out"].reshape(_OUT)
```

```python
from contextlib import ExitStack

import concourse.bass as bass
from concourse import mybir

F32 = mybir.dt.float32
F32R = mybir.dt.float32r
BF16 = mybir.dt.bfloat16
I32 = mybir.dt.int32
U32 = mybir.dt.uint32
ALU = mybir.AluOpType
ACT = mybir.ActivationFunctionType
AX = mybir.AxisListType

P = 128
N, D, E, F = 4096, 256, 8, 1024
HD = 16
KD, FB = D // P, F // P
T = N // P
TC = 4
C = T // TC
CW = TC * P
CAP = int(N / E * 1.25) + 1
SL = CAP + CAP % 2
ST = -(-SL // P)
TAIL = SL - (ST - 1) * P
GA = 3
GROUPS = ((0, GA * P, 0, GA), (GA * P, SL, GA, ST))
HW = GROUPS[0][1]
MEAN, RSTD, WGT, TOK, ROW = D, D + 1, D + 2, D + 3, D + 4
EPS = 1e-5
FAR = 1.0e6
NH, NRO, NY = 4, 3, ST
HU = 2 * FB


def macaron(nc, x, w12, b1, b2, wa, bqkv, bo, wg, out):
    with ExitStack() as ctx:
        def sb(name, shape, dt=F32):
            return ctx.enter_context(nc.sbuf_tensor(name, shape, dt))

        def sem(name):
            return ctx.enter_context(nc.semaphore(name))

        slots = nc.dram_tensor("slots", (E * SL, ROW), F32, kind="Internal").ap()
        x1 = nc.dram_tensor("x1", (N, D), F32, kind="Internal").ap()
        bank = [ctx.enter_context(nc.psum_tensor(f"bank{i}", [P, 512], F32)) for i in range(8)]

        xe = sb("xe", [P, T, ROW])
        raw1, raw2 = sb("raw1", [P, KD * F]), sb("raw2", [P, FB * D])
        w1h, w1l = sb("w1h", [P, 2, KD * F], F32R), sb("w1l", [P, 2, KD * F], F32R)
        w2h, w2l = sb("w2h", [P, 2, FB * D], F32R), sb("w2l", [P, 2, FB * D], F32R)
        hi_part, lo_part = sb("hi_part", [P, FB * SL], F32R), sb("lo_part", [P, FB * SL], F32R)
        zth, ztl = sb("zth", [P, KD, SL], F32R), sb("ztl", [P, KD, SL], F32R)
        ident, upto_f, ones_f, head_f = (sb(n, [P, P]) for n in ("ident", "upto_f", "ones_f", "head_f"))
        upto, ones = sb("upto", [P, P], BF16), sb("ones", [P, P], BF16)
        head = sb("head", [P, P], F32R)
        wgs = sb("wgs", [P, KD, E])
        b1s = sb("b1s", [P, E * FB])
        bqs = sb("bqs", [P, 3, KD])
        bos = sb("bos", [P, D])
        half = sb("half", [P, TC])
        first_code = sb("first_code", [P, E])
        code_i = sb("code_i", [P, E], I32)
        slot_pos = sb("slot_pos", [P, ST])
        pos_i = sb("pos_i", [P, ST], I32)
        tok_i = sb("tok_i", [P, T], I32)
        zero_row = sb("zero_row", [P, ROW])
        stats = sb("stats", [P, 2, TC, 6])
        dlt, code, ranks = (sb(n, [P, TC, E]) for n in ("dlt", "code", "ranks"))
        hot = sb("hot", [P, TC, E], BF16)
        col = sb("col", [P, 8, TC])
        base = sb("base", [P, E])
        unused = sb("unused", [P, E, ST])
        slot_i = sb("slot_i", [P, T], U32)
        tok_idx = sb("tok_idx", [P, 2, ST], U32)

        room = {}

        def cut(t, n):
            a = room.get(t.name, 0)
            room[t.name] = a + n
            return t[:, a:a + n]

        arena = sb("arena", [P, 7 * KD * CW])
        za, zr = (cut(arena, TC * D).rearrange("p (t d) -> p t d", t=TC) for _ in range(2))
        zrt, sqq, sqk, vb, ob = (cut(arena, KD * CW).rearrange("p (k n) -> p k n", k=KD) for _ in range(5))
        lent = xe[:].rearrange("p t c -> p (t c)")
        spot = [0]

        def lend(n, inner):
            a = spot[0]
            spot[0] += n * inner
            assert spot[0] <= T * ROW
            return lent[:, a:spot[0]].rearrange("p (b n) -> p b n", b=n)

        xs = lend(2 * ST, ROW).rearrange("p (b t) c -> p b t c", b=2)
        hbuf, zs, b2s, ro, xb = lend(NH, HW), lend(GA, D), lend(2, D), lend(NRO, D), lend(2, D)

        def cut_r(t, a, n):
            return t[:, a:a + n].rearrange("p (k n) -> p k n", k=KD)

        wah, wal = (w[:, 1, :].rearrange("p (k m d) -> p k m d", k=KD, m=4) for w in (w1h, w1l))

        zh = [cut_r(hi_part, b * KD * CW, KD * CW) for b in range(2)]
        zl = [cut_r(lo_part, b * KD * CW, KD * CW) for b in range(2)]
        eh, el = cut_r(hi_part, 2 * KD * CW, KD * CW), cut_r(lo_part, 2 * KD * CW, KD * CW)
        oh, ol = cut_r(hi_part, 3 * KD * CW, KD * CW), cut_r(lo_part, 3 * KD * CW, KD * CW)
        hh = hi_part[:].rearrange("p (f n) -> p f n", f=FB)
        hl = lo_part[:].rearrange("p (f n) -> p f n", f=FB)
        logits = bank[7][:, 0:TC * E].rearrange("p (t e) -> p t e", t=TC)
        ranks_ps = bank[5][:, 0:TC * E].rearrange("p (t e) -> p t e", t=TC)
        total_ps = bank[5][:, TC * E:TC * E + E]

        s_x = [sem(f"s_x{c}") for c in range(C)]
        s_small = sem("s_small")
        s_wa = sem("s_wa")
        s_shape = sem("s_shape")
        s_const = sem("s_const")
        s_conv = sem("s_conv")
        s_zero = sem("s_zero")
        s_init = sem("s_init")
        s_wah, s_wal = sem("s_wah"), sem("s_wal")
        r_st, r_ag, r_ve, r_rs, r_z = (sem(f"r_{n}") for n in ("st", "ag", "ve", "rs", "z"))
        a_st, a_ag, a_ve, a_rs, a_z = (sem(f"a_{n}") for n in ("st", "ag", "ve", "rs", "z"))
        r_t, r_tc, r_lg = sem("r_t"), sem("r_tc"), sem("r_lg")
        rt_a, rt_b, rt_d, rt_e, rt_hot, rt_cnt, rt_idx, rt_used = (
            sem(f"rt_{n}") for n in ("a", "b", "d", "e", "hot", "cnt", "idx", "used"))
        s_disp = sem("s_disp")
        a_t, a_zh, a_zl, a_bo = sem("a_t"), sem("a_zh"), sem("a_zl"), sem("a_bo")
        a_qkv, a_ev, a_pair, a_exp, a_eh, a_el = (
            sem(f"a_{n}") for n in ("qkv", "ev", "pair", "exp", "eh", "el"))
        a_cf, a_o, a_oh, a_ol, a_y, a_x2 = (sem(f"a_{n}") for n in ("cf", "o", "oh", "ol", "y", "x2"))
        s_x2st = sem("s_x2st")
        e_raw1, e_raw2 = sem("e_raw1"), sem("e_raw2")
        e_w1h, e_w1l, e_w2h, e_w2l = sem("e_w1h"), sem("e_w1l"), sem("e_w2h"), sem("e_w2l")
        e_xs, e_b2 = [sem("e_xs0"), sem("e_xs1")], [sem("e_b20"), sem("e_b21")]
        e_z, e_tz, e_zh, e_zl = (sem(f"e_{n}") for n in ("z", "tz", "zh", "zl"))
        e_l1, e_g, e_hh, e_hl = sem("e_l1"), sem("e_g"), sem("e_hh"), sem("e_hl")
        e_y, e_xb, e_ro, e_idx = sem("e_y"), sem("e_xb"), sem("e_ro"), sem("e_idx")
        e_out = [sem(f"e_out{i}") for i in range(NRO)]

        x_rows = x.rearrange("(p t) d -> p t d", p=P)
        x1_rows = x1.rearrange("(p t) d -> p t d", p=P)
        out_rows = out.rearrange("(p t) d -> p t d", p=P)

        def after(e, s, n):
            if n > 0:
                e.wait_ge(s, n)

        block = ctx.enter_context(nc.Block())

        @block.sync
        def _(sp):
            def tiles(c):
                return slice(TC * c, TC * c + TC)

            zeroed = slots.rearrange("(p a) c -> p a c", p=48)
            cuts = [(E * SL // 48) * i // C for i in range(C + 1)]
            for c in range(C):
                sp.dma_start(xe[:, tiles(c), 0:D], x_rows[:, tiles(c)]).then_inc(s_x[c], 16)
                if c == 0:
                    for dst, src in ((wgs, wg), (b1s, b1), (bqs, bqkv)):
                        sp.dma_start(dst[:], src).then_inc(s_small, 16)
                    sp.dma_start(bos[:], bo.partition_broadcast(P)[:, 0, :]).then_inc(s_small, 16)
                    sp.wait_ge(s_const, 1)
                a, b = cuts[c], cuts[c + 1]
                sp.dma_start(zeroed[:, a:b], zero_row[0:48, None, :].broadcast_to([48, b - a, ROW])).then_inc(s_zero, 16)

            def weights1(g):
                after(sp, e_w1l, KD * g)
                sp.dma_start(raw1[:], w12[g % E, :, 0:KD * F]).then_inc(e_raw1, 16)

            def weights2(g):
                after(sp, e_w2l, KD * g)
                sp.dma_start(raw2[:], w12[g % E, :, KD * F:]).then_inc(e_raw2, 16)

            weights1(0)
            weights2(0)
            for c in range(C):
                sp.wait_ge(s_x[c], 16)
                sp.dma_start(x1_rows[:, tiles(c)], xe[:, tiles(c), 0:D]).then_inc(s_init, 16)

            def rows_of(g):
                e, b = g % E, g % 2
                if e == 0:
                    sp.wait_ge(s_disp, 16 * T * (g // E + 1))
                    sp.wait_ge((s_init, s_x2st)[g // E], 16 * C)
                if e >= 2:
                    sp.wait_ge(e_ro, NY * (g - 1))
                else:
                    sp.wait_ge(rt_used, g // E + 1)
                base = e * SL
                full = (ST - 1) * P
                sp.dma_start(xs[:, b, 0:ST - 1, :],
                             slots[base:base + full].rearrange("(j p) c -> p j c", p=P)).then_inc(e_xs[b], 16)
                sp.dma_start(xs[0:TAIL, b, ST - 1, :], slots[base + full:base + SL]).then_inc(e_xs[b], 16)
                sp.dma_start(b2s[:, b, :], b2[e:e + 1].partition_broadcast(P)[:, 0, :]).then_inc(e_b2[b], 16)

            for ffn in range(2):
                g0 = E * ffn
                rows_of(g0)
                rows_of(g0 + 1)
                for e in range(E):
                    g = g0 + e
                    if g + 1 < 2 * E:
                        weights1(g + 1)
                        weights2(g + 1)
                    if e + 1 == E and ffn == 0:
                        sp.wait_ge(e_w1l, KD * (E + 1))
                        sp.dma_start(raw1[:], wa).then_inc(s_wa, 16)
                    if e + 2 < E:
                        rows_of(g + 2)
                if ffn == 0:
                    for i in range(NRO):
                        sp.wait_ge(e_out[i], 16 * (E * NY // NRO))
                    for c in range(C):
                        sp.dma_start(xe[:, tiles(c), 0:D], x1_rows[:, tiles(c)]).then_inc(s_x[c], 16)
                    for c in range(C):
                        sp.wait_ge(a_x2, 2 * (c + 1))
                        sp.dma_start(out_rows[:, tiles(c)], xe[:, tiles(c), 0:D]).then_inc(s_x2st, 16)
            for i in range(NRO):
                sp.wait_ge(e_out[i], 16 * (2 * E * NY // NRO))

        @block.gpsimd
        def _(pool):
            g_ = nc.gpsimd
            g_.memset(zero_row[:], 0.0).then_inc(s_const, 1)
            g_.memset(ident[:], 0.0)
            g_.memset(ones_f[:], 1.0)
            g_.memset(upto_f[:], 1.0)
            g_.memset(head_f[:], 1.0)
            g_.memset(half[:], -0.5)
            g_.memset(base[:], 0.0)
            g_.iota(tok_i[:], pattern=[[1, T]], base=0, channel_multiplier=T)
            g_.iota(pos_i[:], pattern=[[P, ST]], base=0, channel_multiplier=1)
            g_.iota(code_i[:], pattern=[[-1, E]], base=E, channel_multiplier=0).then_inc(s_shape, 1)
            pool.wait_ge(s_shape, 1)
            g_.affine_select(out=ident[:], in_=ident[:], compare_op=ALU.not_equal, fill=1.0, base=0,
                             pattern=[[-1, P]], channel_multiplier=1)
            g_.affine_select(out=upto_f[:], in_=upto_f[:], compare_op=ALU.is_ge, fill=0.0, base=0,
                             pattern=[[1, P]], channel_multiplier=-1)
            blk = head_f[:].rearrange("p (h d) -> p h d", d=HD)
            g_.affine_select(out=blk, in_=blk, compare_op=ALU.is_ge, fill=0.0, base=0,
                             pattern=[[-HD, P // HD], [0, HD]], channel_multiplier=1).then_inc(s_shape, 1)
            pool.wait_ge(s_shape, 2)
            g_.affine_select(out=blk, in_=blk, compare_op=ALU.is_ge, fill=0.0, base=HD - 1,
                             pattern=[[HD, P // HD], [0, HD]], channel_multiplier=-1).then_inc(s_const, 1)

            def rstd(ve, rs, c, n):
                pool.wait_ge(ve, n + 1)
                v = xe[:, TC * c:TC * c + TC, RSTD]
                g_.tensor_tensor(v, v, half[:], ALU.pow).then_inc(rs, 1)

            def dispatch(c, n):
                pool.wait_ge(rt_idx, n + 1)
                if n == 0:
                    pool.wait_ge(s_zero, 16 * C)
                for t in range(TC * c, TC * c + TC):
                    g_.indirect_dma_start(out=slots, out_offset=bass.IndirectOffsetOnAxis(ap=slot_i[:, t:t + 1], axis=0),
                                          in_=xe[:, t, :], in_offset=None, bounds_check=E * SL - 1,
                                          oob_is_err=False).then_inc(s_disp, 16)

            def results(ffn):
                dst = (x1, out)[ffn]
                pool.wait_ge((s_init, s_x2st)[ffn], 16 * C)
                for y in range(E * NY):
                    yy = ffn * E * NY + y
                    g, j = yy // NY, yy % NY
                    rows = P if j < ST - 1 else TAIL
                    pool.wait_ge(e_idx, 2 * (g + 1))
                    pool.wait_ge(e_ro, yy + 1)
                    g_.indirect_dma_start(out=dst, out_offset=bass.IndirectOffsetOnAxis(
                        ap=tok_idx[0:rows, g % 2, j:j + 1], axis=0), in_=ro[0:rows, yy % NRO, :], in_offset=None,
                        bounds_check=N - 1, oob_is_err=False).then_inc(e_out[yy % NRO], 16)

            for c in range(C + 3):
                if c < C:
                    rstd(r_ve, r_rs, c, c)
                if c >= 3:
                    dispatch(c - 3, c - 3)
            results(0)

            def add_bo(c):
                pool.wait_ge(a_z, c + 1)
                for t in range(TC * c, TC * c + TC):
                    i = g_.tensor_tensor(xe[:, t, 0:D], xe[:, t, 0:D], bos[:], ALU.add)
                i.then_inc(a_bo, 1)

            for s in range(-2, C + 4):
                if 0 <= s + 1 < C:
                    add_bo(s + 1)
                if 0 <= s + 2 < C:
                    rstd(a_ve, a_rs, s + 2, s + 2)
                if 0 <= s - 1 < C:
                    rstd(r_ve, r_rs, s - 1, C + s - 1)
                if 0 <= s - 4 < C:
                    dispatch(s - 4, C + s - 4)
            results(1)

        @block.scalar
        def _(act):
            s_ = nc.scalar

            def router_copy(c, ffn):
                n = C * ffn + c
                for k in range(KD):
                    act.wait_ge(r_t, KD * n + k + 1)
                    after(act, r_lg, n)
                    s_.copy(zrt[:, k, :], bank[k][:]).then_inc(r_tc, 1)

            def router_exp(n):
                act.wait_ge(rt_d, n + 1)
                s_.activation(dlt[:], dlt[:], ACT.Exp).then_inc(rt_e, 1)

            def gelu(g, gi, fs):
                c0, c1, t0, t1 = GROUPS[gi]
                for f in fs:
                    u = HU * g + FB * gi + f
                    h = hbuf[:, u % NH, 0:c1 - c0]
                    act.wait_ge(e_l1, u + 1)
                    after(act, e_hl, u + 1 - NH)
                    e = g % E
                    s_.activation(h, bank[2 + u % 4][:, 0:c1 - c0], ACT.Gelu,
                                  bias=b1s[:, e * FB + f:e * FB + f + 1]).then_inc(e_g, 1)
                    act.wait_ge(e_g, u + 1)
                    after(act, e_y, NY * (g - 1) + t1)
                    s_.copy(hh[:, f, c0:c1], h).then_inc(e_hh, 1)

            def slots_hi(g, gi):
                c0, c1, t0, t1 = GROUPS[gi]
                act.wait_ge(e_tz, ST * g + t1)
                after(act, e_l1, HU * (g - 1) + FB * (gi + 1))
                for k in range(KD):
                    s_.copy(zth[:, k, c0:c1], bank[k][:, 0:c1 - c0]).then_inc(e_zh, 1)

            def w1_hi(g, k):
                act.wait_ge(e_raw1, 16 * (g + 1))
                after(act, e_l1, HU * (g - 1))
                if g == E + 1:
                    act.wait_ge(a_y, 2 * C)
                ks = slice(k * F, (k + 1) * F)
                s_.copy(w1h[:, g % 2, ks], raw1[:, ks]).then_inc(e_w1h, 1)

            def w2_hi(g, k):
                act.wait_ge(e_raw2, 16 * (g + 1))
                after(act, e_y, NY * (g - 1))
                ks = slice(k * FB * D // 2, (k + 1) * FB * D // 2)
                s_.copy(w2h[:, g % 2, ks], raw2[:, ks]).then_inc(e_w2h, 1)

            act.wait_ge(s_small, 64)
            for c in range(C + 1):
                if c >= 1:
                    router_exp(c - 1)
                if c < C:
                    router_copy(c, 0)
            for k in range(KD):
                w1_hi(0, k)
            for k in range(KD):
                w2_hi(0, k)
            for ffn in range(2):
                g0 = E * ffn
                slots_hi(g0, 0)
                gelu(g0, 0, range(0, 3))
                gelu(g0, 0, range(3, 8))
                slots_hi(g0, 1)
                for e in range(E):
                    g, more = g0 + e, e + 1 < E
                    gelu(g, 1, range(0, 3))
                    if g + 1 < 2 * E:
                        w1_hi(g + 1, 0)
                    gelu(g, 1, range(3, 6))
                    if g + 1 < 2 * E:
                        w1_hi(g + 1, 1)
                    gelu(g, 1, range(6, 8))
                    if more:
                        slots_hi(g + 1, 0)
                        gelu(g + 1, 0, range(0, 3))
                    if g + 1 < 2 * E:
                        w2_hi(g + 1, 0)
                    if more:
                        gelu(g + 1, 0, range(3, 6))
                    if g + 1 < 2 * E:
                        w2_hi(g + 1, 1)
                    if more:
                        gelu(g + 1, 0, range(6, 8))
                        slots_hi(g + 1, 1)
                if ffn == 1:
                    break

                act.wait_ge(s_wa, 16)
                act.wait_ge(e_l1, HU * E)
                s_.copy(w1h[:, 1, :], raw1[:]).then_inc(s_wah, 1)

                def z_hi(c):
                    for k in range(KD):
                        act.wait_ge(a_t, KD * c + k + 1)
                        after(act, a_qkv, 6 * (c - 1))
                        s_.copy(zh[c % 2][:, k, :], bank[k][:]).then_inc(a_zh, 1)

                def o_hi(c, m):
                    act.wait_ge(a_o, KD * c + m + 1)
                    after(act, a_y, 2 * c)
                    s_.copy(oh[:, m, :], ob[:, m, :]).then_inc(a_oh, 1)

                def squares(c, m):
                    for i, (sq, which) in enumerate(((sqq, 0), (sqk, 1))):
                        u = 6 * c + 2 * m + i
                        act.wait_ge(a_qkv, u + 1)
                        after(act, a_el, KD * (c - 1) + m + 1)
                        s_.activation(sq[:, m, :], bank[2 + u % 3][:], ACT.Square,
                                      bias=bqs[:, which, m:m + 1]).then_inc(a_ev, 1)

                def exp_hi(c, m):
                    act.wait_ge(a_pair, KD * c + m + 1)
                    s_.activation(sqq[:, m, :], sqq[:, m, :], ACT.Exp, scale=-0.5).then_inc(a_exp, 1)
                    act.wait_ge(a_exp, KD * c + m + 1)
                    after(act, a_cf, KD * c)
                    s_.copy(eh[:, m, :], sqq[:, m, :]).then_inc(a_eh, 1)

                def values(c):
                    for m in range(KD):
                        u = 6 * c + 4 + m
                        act.wait_ge(a_qkv, u + 1)
                        after(act, a_o, KD * c)
                        s_.activation(vb[:, m, :], bank[2 + u % 3][:], ACT.Identity,
                                      bias=bqs[:, 2, m:m + 1]).then_inc(a_ev, 1)

                for s in range(-1, C + 4):
                    now, prev = 0 <= s < C, 0 <= s - 1 < C
                    if 0 <= s + 1 < C:
                        z_hi(s + 1)
                    if 0 <= s - 3 < C:
                        router_exp(C + s - 3)
                    if prev:
                        o_hi(s - 1, 0)
                    if now:
                        squares(s, 0)
                    if prev:
                        o_hi(s - 1, 1)
                    if now:
                        squares(s, 1)
                        exp_hi(s, 0)
                        values(s)
                        exp_hi(s, 1)
                    if 0 <= s - 2 < C:
                        router_copy(s - 2, 1)

        @block.vector
        def _(dve):
            v_ = nc.vector
            pieces = lambda a: a.rearrange("p k m d -> p (k m d)")

            def ln_stats(c, n, st, ag, ve, par):
                for i in range(TC):
                    v_.bn_stats(stats[:, par, i, :], xe[:, TC * c + i, 0:D]).then_inc(st, 1)
                for i in range(TC):
                    dve.wait_ge(st, TC * n + i + 1)
                    v_.bn_aggr(xe[:, TC * c + i, MEAN:RSTD + 1], stats[:, par, i, :]).then_inc(ag, 1)
                dve.wait_ge(ag, TC * (n + 1))
                v = xe[:, TC * c:TC * c + TC, RSTD]
                v_.tensor_scalar(v, v, EPS, None, ALU.add).then_inc(ve, 1)

            def ln_norm(c, n, rs, z, zdone):
                dve.wait_ge(rs, n + 1)
                for i in range(TC):
                    t = TC * c + i
                    q = v_.tensor_scalar(z[:, i, :], xe[:, t, 0:D], xe[:, t, MEAN:MEAN + 1],
                                         xe[:, t, RSTD:RSTD + 1], ALU.subtract, ALU.mult)
                q.then_inc(zdone, 1)

            NA, NB = 4, 10

            def linked(s, n, per):
                k = [per * n]

                def link(i):
                    k[0] += 1
                    i.then_inc(s, 1)
                    dve.wait_ge(s, k[0])

                return link

            def route_pick(n):
                link = linked(rt_a, n, NA)
                dve.wait_ge(r_lg, n + 1)
                link(v_.tensor_reduce(col[:, 0, :], logits, AX.X, ALU.max))
                link(v_.tensor_tensor(dlt[:], logits, col[:, 0, :].unsqueeze(2).broadcast_to([P, TC, E]),
                                      ALU.subtract))
                v_.scalar_tensor_tensor(out=code[:], in0=dlt[:], scalar=0.0,
                                        in1=first_code[:].unsqueeze(1).broadcast_to([P, TC, E]),
                                        op0=ALU.is_ge, op1=ALU.mult).then_inc(rt_d, 1)
                dve.wait_ge(rt_d, n + 1)
                link(v_.tensor_reduce(col[:, 1, :], code[:], AX.X, ALU.max))
                v_.tensor_tensor(hot[:], code[:], col[:, 1, :].unsqueeze(2).broadcast_to([P, TC, E]),
                                 ALU.is_equal).then_inc(rt_hot, 1)
                dve.wait_ge(rt_e, n + 1)
                link(v_.tensor_reduce(col[:, 2, :], dlt[:], AX.X, ALU.add))
                v_.reciprocal(col[:, 3, :], col[:, 2, :]).then_inc(rt_b, 1)

            def route_slot(c, n):
                link = linked(rt_b, n, NB)
                dve.wait_ge(rt_b, NB * n + 1)
                v_.tensor_scalar(xe[:, TC * c:TC * c + TC, WGT], col[:, 3, :], 0.5, None, ALU.mult).then_inc(rt_b, 1)
                dve.wait_ge(rt_cnt, n + 1)
                v_.tensor_tensor(ranks[:], ranks_ps, base[:].unsqueeze(1).broadcast_to([P, TC, E]),
                                 ALU.add).then_inc(rt_b, 1)
                v_.tensor_scalar(col[:, 4, :], col[:, 1, :], -float(SL), float(E * SL - 1), ALU.mult,
                                 ALU.add).then_inc(rt_b, 1)
                dve.wait_ge(rt_b, NB * n + 4)
                v_.tensor_tensor(base[:], base[:], total_ps, ALU.add).then_inc(rt_b, 1)
                v_.tensor_tensor(ranks[:], ranks[:], hot[:], ALU.mult).then_inc(rt_b, 1)
                dve.wait_ge(rt_b, NB * n + 6)
                v_.tensor_reduce(col[:, 5, :], ranks[:], AX.X, ALU.add).then_inc(rt_b, 1)
                dve.wait_ge(rt_b, NB * n + 7)
                v_.tensor_scalar(col[:, 6, :], col[:, 5, :], float(CAP), FAR, ALU.is_gt, ALU.mult).then_inc(rt_b, 1)
                v_.tensor_tensor(col[:, 7, :], col[:, 5, :], col[:, 4, :], ALU.add).then_inc(rt_b, 1)
                dve.wait_ge(rt_b, NB * n + 9)
                v_.tensor_tensor(slot_i[:, TC * c:TC * c + TC], col[:, 7, :], col[:, 6, :], ALU.add).then_inc(rt_b, 1)
                dve.wait_ge(rt_b, NB * n + 10)
                v_.tensor_copy(xe[:, TC * c:TC * c + TC, TOK], tok_i[:, TC * c:TC * c + TC]).then_inc(rt_idx, 1)

            def route_end(ffn):
                v_.tensor_scalar(col[:].rearrange("p a b -> p (a b)")[:, 0:E], base[:], float(CAP), None,
                                 ALU.min).then_inc(rt_used, 1)
                dve.wait_ge(rt_used, 4 * ffn + 1)
                v_.tensor_tensor(unused[:], slot_pos[:].unsqueeze(1).broadcast_to([P, E, ST]),
                                 col[:].rearrange("p a b -> p (a b)")[:, 0:E].unsqueeze(2).broadcast_to([P, E, ST]),
                                 ALU.is_ge).then_inc(rt_used, 1)
                dve.wait_ge(rt_used, 4 * ffn + 2)
                v_.tensor_scalar(unused[:], unused[:], FAR, None, ALU.mult).then_inc(rt_used, 1)
                v_.memset(base[:], 0.0).then_inc(rt_used, 1)

            def w1_lo(g, k):
                dve.wait_ge(e_w1h, KD * g + k + 1)
                ks = slice(k * F, (k + 1) * F)
                v_.tensor_tensor(w1l[:, g % 2, ks], raw1[:, ks], w1h[:, g % 2, ks].bitcast(F32),
                                 ALU.subtract).then_inc(e_w1l, 1)

            def w2_lo(g, k):
                dve.wait_ge(e_w2h, KD * g + k + 1)
                ks = slice(k * FB * D // 2, (k + 1) * FB * D // 2)
                v_.tensor_tensor(w2l[:, g % 2, ks], raw2[:, ks], w2h[:, g % 2, ks].bitcast(F32),
                                 ALU.subtract).then_inc(e_w2l, 1)

            def slots_z(g, gi):
                b, (c0, c1, t0, t1) = g % 2, GROUPS[gi]
                dve.wait_ge(e_xs[b], 32 * (g // 2 + 1))
                after(dve, e_tz, ST * g + t0)
                for j in range(t0, t1):
                    rows = P if j < ST - 1 else TAIL
                    v_.tensor_scalar(zs[0:rows, j - t0, :], xs[0:rows, b, j, 0:D], xs[0:rows, b, j, MEAN:MEAN + 1],
                                     xs[0:rows, b, j, RSTD:RSTD + 1], ALU.subtract, ALU.mult).then_inc(e_z, 1)

            def slots_lo(g, gi):
                c0, c1, t0, t1 = GROUPS[gi]
                for k in range(KD):
                    n = (2 * g + gi) * KD + k
                    dve.wait_ge(e_zh, n + 1)
                    v_.tensor_tensor(ztl[:, k, c0:c1], bank[k][:, 0:c1 - c0], zth[:, k, c0:c1].bitcast(F32),
                                     ALU.subtract).then_inc(e_zl, 1)

            def goals(g):
                b, e = g % 2, g % E
                dve.wait_ge(rt_used, 4 * (g // E + 1))
                if g >= 2:
                    for i in range(NRO):
                        dve.wait_ge(e_out[i], 16 * NY // NRO * (g - 1))
                v_.tensor_tensor(tok_idx[:, b, 0:ST - 1], xs[:, b, 0:ST - 1, TOK], unused[:, e, 0:ST - 1],
                                 ALU.add).then_inc(e_idx, 1)
                v_.tensor_tensor(tok_idx[0:TAIL, b, ST - 1:ST], xs[0:TAIL, b, ST - 1, TOK:TOK + 1],
                                 unused[0:TAIL, e, ST - 1:ST], ALU.add).then_inc(e_idx, 1)

            def hidden(g, gi, fs):
                c0, c1, t0, t1 = GROUPS[gi]
                for f in fs:
                    u = HU * g + FB * gi + f
                    dve.wait_ge(e_hh, u + 1)
                    v_.tensor_tensor(hl[:, f, c0:c1], hbuf[:, u % NH, 0:c1 - c0], hh[:, f, c0:c1].bitcast(F32),
                                     ALU.subtract).then_inc(e_hl, 1)

            def result(g, j):
                b, yy = g % 2, NY * g + j
                rows = P if j < ST - 1 else TAIL
                w = xs[0:rows, b, j, WGT:WGT + 1]
                if j == 0:
                    dve.wait_ge(e_b2[b], 16 * (g // 2 + 1))
                v_.scalar_tensor_tensor(out=xb[0:rows, yy % 2, :], in0=b2s[0:rows, b, :], scalar=w,
                                        in1=xs[0:rows, b, j, 0:D], op0=ALU.mult, op1=ALU.add).then_inc(e_xb, 1)
                dve.wait_ge(e_xb, yy + 1)
                dve.wait_ge(e_y, yy + 1)
                after(dve, e_out[yy % NRO], 16 * (yy // NRO))
                v_.scalar_tensor_tensor(out=ro[0:rows, yy % NRO, :], in0=bank[6 + yy % 2][0:rows, 0:D], scalar=w,
                                        in1=xb[0:rows, yy % 2, :], op0=ALU.mult, op1=ALU.add).then_inc(e_ro, 1)

            dve.wait_ge(s_const, 2)
            v_.tensor_copy(head[:], head_f[:])
            v_.tensor_copy(upto[:], upto_f[:])
            v_.tensor_copy(ones[:], ones_f[:])
            v_.tensor_copy(slot_pos[:], pos_i[:])
            v_.tensor_copy(first_code[:], code_i[:]).then_inc(s_conv, 1)
            dve.wait_ge(s_conv, 1)
            for s in range(-1, C + 2):
                if 0 <= s + 1 < C:
                    dve.wait_ge(s_x[s + 1], 16)
                    after(dve, r_ag, TC * (s + 1))
                    ln_stats(s + 1, s + 1, r_st, r_ag, r_ve, 0)
                if 0 <= s < C:
                    after(dve, r_t, KD * s)
                    ln_norm(s, s, r_rs, zr, r_z)
                if 0 <= s - 1 < C:
                    route_pick(s - 1)
                if 0 <= s - 1 < C:
                    route_slot(s - 1, s - 1)
            for k in range(KD):
                w1_lo(0, k)
            for k in range(KD):
                w2_lo(0, k)
            for ffn in range(2):
                route_end(ffn)
                g0 = E * ffn
                slots_z(g0, 0)
                goals(g0)
                slots_lo(g0, 0)
                hidden(g0, 0, range(0, 3))
                slots_z(g0, 1)
                hidden(g0, 0, range(3, 8))
                slots_lo(g0, 1)
                for e in range(E):
                    g, more = g0 + e, e + 1 < E
                    hidden(g, 1, range(0, 3))
                    if more:
                        slots_z(g + 1, 0)
                        goals(g + 1)
                    result(g, 0)
                    hidden(g, 1, range(3, 6))
                    if g + 1 < 2 * E:
                        w1_lo(g + 1, 0)
                    result(g, 1)
                    hidden(g, 1, range(6, 8))
                    if g + 1 < 2 * E:
                        w1_lo(g + 1, 1)
                    if more:
                        slots_lo(g + 1, 0)
                    result(g, 2)
                    if more:
                        hidden(g + 1, 0, range(0, 3))
                        slots_z(g + 1, 1)
                    result(g, 3)
                    if more:
                        hidden(g + 1, 0, range(3, 6))
                    if g + 1 < 2 * E:
                        w2_lo(g + 1, 0)
                    result(g, 4)
                    if more:
                        hidden(g + 1, 0, range(6, 8))
                    if g + 1 < 2 * E:
                        w2_lo(g + 1, 1)
                    if more:
                        slots_lo(g + 1, 1)
                    result(g, 5)
                if ffn == 1:
                    break

                dve.wait_ge(s_wah, 1)
                v_.tensor_tensor(w1l[:, 1, :], raw1[:], w1h[:, 1, :].bitcast(F32), ALU.subtract).then_inc(s_wal, 1)

                def z_lo(c):
                    for m in range(KD):
                        dve.wait_ge(a_zh, KD * c + m + 1)
                        v_.tensor_tensor(zl[c % 2][:, m, :], bank[m][:], zh[c % 2][:, m, :].bitcast(F32),
                                         ALU.subtract).then_inc(a_zl, 1)

                def weigh(c, m):
                    dve.wait_ge(a_cf, KD * c + m + 1)
                    dve.wait_ge(a_ev, 6 * c + 5 + m)
                    after(dve, a_ol, KD * (c - 1) + m + 1)
                    after(dve, a_oh, KD * (c - 1) + m + 1)
                    v_.tensor_tensor(ob[:, m, :], bank[5][:], vb[:, m, :], ALU.mult).then_inc(a_o, 1)

                def o_lo(c, m):
                    dve.wait_ge(a_oh, KD * c + m + 1)
                    v_.tensor_tensor(ol[:, m, :], ob[:, m, :], oh[:, m, :].bitcast(F32),
                                     ALU.subtract).then_inc(a_ol, 1)

                def pair(c, m):
                    dve.wait_ge(a_ev, 6 * c + 2 * m + 2)
                    v_.tensor_tensor(sqq[:, m, :], sqq[:, m, :], sqk[:, m, :], ALU.add).then_inc(a_pair, 1)

                def e_lo(c, m):
                    dve.wait_ge(a_eh, KD * c + m + 1)
                    v_.tensor_tensor(el[:, m, :], sqq[:, m, :], eh[:, m, :].bitcast(F32),
                                     ALU.subtract).then_inc(a_el, 1)

                def add_y(c, h):
                    dve.wait_ge(a_bo, c + 1)
                    h += 2 * c
                    dve.wait_ge(a_y, h + 1)
                    xt = xe[:, 2 * h:2 * h + 2, 0:D]
                    v_.tensor_tensor(xt, bank[6][:].rearrange("p (t d) -> p t d", t=2), xt,
                                     ALU.add).then_inc(a_x2, 1)

                for s in range(-2, C + 4):
                    now, prev = 0 <= s < C, 0 <= s - 1 < C
                    if 0 <= s + 1 < C:
                        z_lo(s + 1)
                    if 0 <= s - 3 < C:
                        route_pick(C + s - 3)
                    if prev:
                        weigh(s - 1, 0)
                        o_lo(s - 1, 0)
                    if now:
                        pair(s, 0)
                    if prev:
                        weigh(s - 1, 1)
                        o_lo(s - 1, 1)
                    if now:
                        pair(s, 1)
                    if 0 <= s + 2 < C:
                        dve.wait_ge(s_x[s + 2], 32)
                        ln_stats(s + 2, s + 2, a_st, a_ag, a_ve, 1)
                    if now:
                        e_lo(s, 0)
                    if 0 <= s - 3 < C:
                        route_slot(s - 3, C + s - 3)
                    if prev:
                        add_y(s - 1, 0)
                    if now:
                        e_lo(s, 1)
                    if prev:
                        add_y(s - 1, 1)
                        dve.wait_ge(a_x2, 2 * s)
                        ln_stats(s - 1, C + s - 1, r_st, r_ag, r_ve, 0)
                    if 0 <= s + 2 < C:
                        after(dve, a_t, KD * (s + 2))
                        ln_norm(s + 2, s + 2, a_rs, za, a_z)
                    if prev:
                        after(dve, r_t, KD * (C + s - 1))
                        ln_norm(s - 1, C + s - 1, r_rs, zr, r_z)

        @block.tensor
        def _(pe):
            t_ = nc.tensor

            def three(o, ah, al, bh, bl, first, last):
                t_.matmul(o, ah, bh, start=first, stop=False)
                t_.matmul(o, ah, bl, start=False, stop=False)
                return t_.matmul(o, al, bh, start=False, stop=last)

            def turn(c, n, z, zdone, done):
                pe.wait_ge(zdone, n + 1)
                for k in range(KD):
                    for i in range(TC):
                        q = t_.transpose(bank[k][:, i * P:(i + 1) * P], z[:, i, k * P:(k + 1) * P], ident[:])
                    q.then_inc(done, 1)

            def router_logits(n):
                pe.wait_ge(r_tc, KD * (n + 1))
                after(pe, rt_d, n)
                for i in range(TC):
                    for k in range(KD):
                        q = t_.matmul(logits[:, i, :], zrt[:, k, i * P:(i + 1) * P], wgs[:, k, :],
                                      start=(k == 0), stop=(k == KD - 1))
                q.then_inc(r_lg, 1)

            def counts(n):
                pe.wait_ge(rt_hot, n + 1)
                after(pe, rt_b, 10 * n)
                h = hot[:].rearrange("p t e -> p (t e)")
                w = TC * E
                t_.matmul(bank[5][:, 0:w], upto[:], h, start=True, stop=False)
                for i in range(1, TC):
                    t_.matmul(bank[5][:, E * i:w], ones[:], h[:, 0:w - E * i], start=False, stop=(i == TC - 1))
                for i in range(TC):
                    q = t_.matmul(total_ps, ones[:], h[:, E * i:E * (i + 1)], start=(i == 0), stop=(i == TC - 1))
                q.then_inc(rt_cnt, 1)

            def slots_t(g, gi):
                c0, c1, t0, t1 = GROUPS[gi]
                after(pe, e_zl, KD * (2 * g + gi))
                for j in range(t0, t1):
                    rows = P if j < ST - 1 else TAIL
                    pe.wait_ge(e_z, ST * g + j + 1)
                    for k in range(KD):
                        q = t_.transpose(bank[k][:, (j - t0) * P:(j - t0) * P + rows],
                                         zs[0:rows, j - t0, k * P:(k + 1) * P], ident[0:rows, 0:rows])
                    q.then_inc(e_tz, 1)

            def layer1(g, gi, fs):
                c0, c1, t0, t1 = GROUPS[gi]
                pe.wait_ge(e_zl, KD * (2 * g + gi + 1))
                pe.wait_ge(e_w1l, KD * (g + 1))
                wh, wl = (w[:, g % 2, :].rearrange("p (k f) -> p k f", k=KD) for w in (w1h, w1l))
                for f in fs:
                    u = HU * g + FB * gi + f
                    after(pe, e_g, u - 3)
                    o = bank[2 + u % 4][:, 0:c1 - c0]
                    for k in range(KD):
                        ks = slice(f * P, (f + 1) * P)
                        q = three(o, wh[:, k, ks], wl[:, k, ks], zth[:, k, c0:c1], ztl[:, k, c0:c1],
                                  k == 0, k == KD - 1)
                    q.then_inc(e_l1, 1)

            def layer2(g, j):
                gi = 0 if j < GA else 1
                yy = NY * g + j
                rows = P if j < ST - 1 else TAIL
                pe.wait_ge(e_hl, HU * g + FB * (gi + 1))
                pe.wait_ge(e_w2l, KD * (g + 1))
                after(pe, e_ro, yy - 1)
                o = bank[6 + yy % 2][0:rows, 0:D]
                wh, wl = (w[:, g % 2, :].rearrange("p (f d) -> p f d", f=FB) for w in (w2h, w2l))
                for f in range(FB):
                    ns = slice(j * P, j * P + rows)
                    q = three(o, hh[:, f, ns], hl[:, f, ns], wh[:, f, :], wl[:, f, :], f == 0, f == FB - 1)
                q.then_inc(e_y, 1)

            pe.wait_ge(s_const, 2)
            pe.wait_ge(s_small, 64)
            pe.wait_ge(s_conv, 1)
            for s in range(C + 1):
                if s < C:
                    after(pe, r_tc, KD * s)
                    turn(s, s, zr, r_z, r_t)
                if s >= 1:
                    counts(s - 1)
                if s < C:
                    router_logits(s)
            for ffn in range(2):
                g0 = E * ffn
                slots_t(g0, 0)
                layer1(g0, 0, range(0, 8))
                slots_t(g0, 1)
                for e in range(E):
                    g, more = g0 + e, e + 1 < E
                    layer1(g, 1, range(0, 3))
                    layer2(g, 0)
                    layer1(g, 1, range(3, 6))
                    layer2(g, 1)
                    layer1(g, 1, range(6, 8))
                    if more:
                        slots_t(g + 1, 0)
                    layer2(g, 2)
                    if more:
                        layer1(g + 1, 0, range(0, 3))
                    layer2(g, 3)
                    if more:
                        layer1(g + 1, 0, range(3, 6))
                    layer2(g, 4)
                    if more:
                        layer1(g + 1, 0, range(6, 8))
                        slots_t(g + 1, 1)
                    layer2(g, 5)
                if ffn == 1:
                    break

                def qkv(c, i):
                    which, m = ((0, 0), (1, 0), (0, 1), (1, 1), (2, 0), (2, 1))[i]
                    u = 6 * c + i
                    pe.wait_ge(a_zl, KD * (c + 1))
                    pe.wait_ge(s_wal, 1)
                    after(pe, a_ev, u - 2)
                    ms = slice(m * P, (m + 1) * P)
                    for k in range(KD):
                        q = three(bank[2 + u % 3][:], wah[:, k, which, ms], wal[:, k, which, ms],
                                  zh[c % 2][:, k, :], zl[c % 2][:, k, :], k == 0, k == KD - 1)
                    q.then_inc(a_qkv, 1)

                def coeff(c, m):
                    pe.wait_ge(a_el, KD * c + m + 1)
                    after(pe, a_o, KD * c + m)
                    if m == 0 and c >= 3:
                        pe.wait_ge(rt_b, 10 * (C + c - 2))
                    t_.matmul(bank[5][:], head[:], eh[:, m, :], start=True, stop=False)
                    t_.matmul(bank[5][:], head[:], el[:, m, :], start=False, stop=True).then_inc(a_cf, 1)

                def project(c, h):
                    pe.wait_ge(a_ol, KD * (c + 1))
                    after(pe, a_x2, 2 * c + h)
                    for i in range(2 * h, 2 * h + 2):
                        for k in range(KD):
                            ns = slice(i * P, (i + 1) * P)
                            q = three(bank[6][:, (i % 2) * D:(i % 2) * D + D], oh[:, k, ns], ol[:, k, ns],
                                      wah[:, k, 3, :], wal[:, k, 3, :], k == 0, k == KD - 1)
                    q.then_inc(a_y, 1)

                for s in range(-1, C + 4):
                    now, prev = 0 <= s < C, 0 <= s - 1 < C
                    if 0 <= s + 1 < C:
                        after(pe, r_tc, KD * (C + s - 2))
                        turn(s + 1, s + 1, za, a_z, a_t)
                    if prev:
                        coeff(s - 1, 0)
                    if now:
                        for i in range(3):
                            qkv(s, i)
                    if prev:
                        coeff(s - 1, 1)
                    if now:
                        for i in range(3, 6):
                            qkv(s, i)
                    if 0 <= s - 3 < C:
                        if prev:
                            pe.wait_ge(a_o, KD * s)
                        counts(C + s - 3)
                    if prev:
                        project(s - 1, 0)
                    if 0 <= s - 2 < C:
                        after(pe, a_zl, KD * min(s + 2, C))
                        turn(s - 2, C + s - 2, zr, r_z, r_t)
                    if prev:
                        project(s - 1, 1)
                    if 0 <= s - 2 < C:
                        router_logits(C + s - 2)


_OUT = (8, 512, 256)


def kernel(L0_attn_x, L0_attn_Wq, L0_attn_bq, L0_attn_Wk, L0_attn_bk, L0_attn_Wv, L0_attn_bv, L0_attn_Wo,
           L0_attn_bo, L0_ffn_wg, L0_ffn_W1, L0_ffn_b1, L0_ffn_W2, L0_ffn_b2):
    import numpy as np
    import concourse.bacc as bacc
    from concourse.bass_utils import run_bass_kernel_spmd

    a = np.ascontiguousarray
    wa = np.stack([L0_attn_Wq, L0_attn_Wk, L0_attn_Wv, L0_attn_Wo], 1)
    w1 = np.asarray(L0_ffn_W1).reshape(E, KD, P, F).transpose(0, 2, 1, 3).reshape(E, P, KD * F)
    w2 = np.asarray(L0_ffn_W2).reshape(E, FB, P, D).transpose(0, 2, 1, 3).reshape(E, P, FB * D)
    arrays = {
        "x": a(np.asarray(L0_attn_x).reshape(T, P, D).transpose(1, 0, 2).reshape(N, D)),
        "w12": a(np.concatenate([w1, w2], 2)),
        "b1": a(np.asarray(L0_ffn_b1).reshape(E, FB, P).transpose(2, 0, 1).reshape(P, E * FB)),
        "b2": a(np.asarray(L0_ffn_b2)),
        "wa": a(wa.reshape(KD, P, 4 * D).transpose(1, 0, 2).reshape(P, KD * 4 * D)),
        "bqkv": a(np.stack([L0_attn_bq, L0_attn_bk, L0_attn_bv]).reshape(3, KD, P).transpose(2, 0, 1)),
        "bo": a(np.asarray(L0_attn_bo).reshape(1, D)),
        "wg": a(np.asarray(L0_ffn_wg).reshape(KD, P, E).transpose(1, 0, 2)),
    }
    nc = bacc.Bacc("TRN2", target_bir_lowering=False, num_devices=1)
    args = [nc.dram_tensor(n, v.shape, mybir.dt.from_np(v.dtype), kind="ExternalInput").ap()
            for n, v in arrays.items()]
    out = nc.dram_tensor("out", (N, D), F32, kind="ExternalOutput").ap()
    macaron(nc, *args, out)
    r = run_bass_kernel_spmd(nc, [arrays], core_ids=[0])
    return a(r.results[0]["out"].reshape(P, T, D).transpose(1, 0, 2)).reshape(_OUT)
```

```python
from contextlib import ExitStack

import concourse.bass as bass
from concourse import mybir

F32 = mybir.dt.float32
F32R = mybir.dt.float32r
BF16 = mybir.dt.bfloat16
I32 = mybir.dt.int32
U32 = mybir.dt.uint32
ALU = mybir.AluOpType
ACT = mybir.ActivationFunctionType
AX = mybir.AxisListType

P = 128
N, D, E, F = 4096, 256, 8, 1024
HD = 16
KD, FB = D // P, F // P
T = N // P
TC = 4
C = T // TC
CW = TC * P
CAP = int(N / E * 1.25) + 1
SL = CAP + CAP % 2
ST = -(-SL // P)
TAIL = SL - (ST - 1) * P
SURE = ST - 2
GA = 2
GROUPS = ((0, GA * P, 0, GA), (GA * P, SL, GA, ST))
HW = SL - GA * P
MEAN, RSTD, WGT, TOK, ROW = D, D + 1, D + 2, D + 3, D + 4
EPS = 1e-5
FAR = 1.0e6
NH, NRO, NY = 4, 3, ST
ZP = 48
PICK, SLOT = 7, 10
HU = 2 * FB
AHEAD = 4
WARM = 9
IDLE = {0: (8, 8, 4), 1: (0, 8, 4)}
EC = 2


def second(engine, count, unit, x, fs):
    with engine.If(count > SURE * P):
        unit(x, 1, fs, SL)
    with engine.Else():
        unit(x, 1, fs, SURE * P)


class Turn:

    def __init__(self, ffn, i, b):
        self.b = b
        self.e = 2 * i + b
        self.n = i + E // 2 * ffn
        self.g = self.n * 2 + b + EC


def turns(ffn, engine):
    with engine.Fori(0, E // 2 - 1) as i:
        yield Turn(ffn, i, 0), Turn(ffn, i, 1), False
        yield Turn(ffn, i, 1), Turn(ffn, i + 1, 0), False
    i = E // 2 - 1
    yield Turn(ffn, i, 0), Turn(ffn, i, 1), False
    yield Turn(ffn, i, 1), Turn(ffn + 1, 0, 0), True


def macaron(nc, x, w12, b1, b2, wa, bqkv, bo, wg, out):
    with ExitStack() as ctx:
        def sb(name, shape, dt=F32):
            return ctx.enter_context(nc.sbuf_tensor(name, shape, dt))

        def sem(name):
            return ctx.enter_context(nc.semaphore(name))

        slots = nc.dram_tensor("slots", (E * SL, ROW), F32, kind="Internal").ap()
        x1 = nc.dram_tensor("x1", (N, D), F32, kind="Internal").ap()
        bank = [ctx.enter_context(nc.psum_tensor(f"bank{i}", [P, 512], F32)) for i in range(8)]

        xe = sb("xe", [P, T, ROW])
        raw1, raw2 = sb("raw1", [P, KD * F]), sb("raw2", [P, FB * D])
        w1h, w1l = sb("w1h", [P, 2, KD * F], F32R), sb("w1l", [P, 2, KD * F], F32R)
        w2h, w2l = sb("w2h", [P, 2, FB * D], F32R), sb("w2l", [P, 2, FB * D], F32R)
        hi_part, lo_part = sb("hi_part", [P, FB * SL], F32R), sb("lo_part", [P, FB * SL], F32R)
        zth, ztl = sb("zth", [P, KD, SL], F32R), sb("ztl", [P, KD, SL], F32R)
        ident, upto_f, ones_f, head_f = (sb(n, [P, P]) for n in ("ident", "upto_f", "ones_f", "head_f"))
        upto, ones = sb("upto", [P, P], BF16), sb("ones", [P, P], BF16)
        wgs = sb("wgs", [P, KD, E])
        b1s = sb("b1s", [P, 2, FB])
        bqs = sb("bqs", [P, 3, KD])
        bos = sb("bos", [P, D])
        half = sb("half", [P, TC])
        spare = sb("spare", [P, 1])
        head_r = sb("head_r", [P, P], F32R)
        first_code = sb("first_code", [P, E])
        code_i = sb("code_i", [P, E], I32)
        slot_pos = sb("slot_pos", [P, ST])
        pos_i = sb("pos_i", [P, ST], I32)
        tok_i = sb("tok_i", [P, T], I32)
        zero_row = sb("zero_row", [P, ROW])
        nbias = sb("nbias", [P, 2, TC])
        stats = sb("stats", [P, 2, TC, 6])
        dlt, code, ranks = (sb(n, [P, TC, E]) for n in ("dlt", "code", "ranks"))
        hot = sb("hot", [P, TC, E], BF16)
        col = sb("col", [P, 8, TC])
        base = sb("base", [P, E])
        unused = sb("unused", [P, E, ST])
        slot_i = sb("slot_i", [P, T], U32)
        tok_idx = sb("tok_idx", [P, 2, ST], U32)
        filled = sb("filled", [P, E], I32)

        room = {}

        def cut(t, n):
            a = room.get(t.name, 0)
            room[t.name] = a + n
            return t[:, a:a + n]

        arena = sb("arena", [P, 7 * KD * CW])
        za, zr = (cut(arena, TC * D).rearrange("p (t d) -> p t d", t=TC) for _ in range(2))
        zrt, sqq, sqk, vb, ob = (cut(arena, KD * CW).rearrange("p (k n) -> p k n", k=KD) for _ in range(5))
        lent = xe[:].rearrange("p t c -> p (t c)")
        spot = [0]

        def lend(n, inner):
            a = spot[0]
            spot[0] += n * inner
            assert spot[0] <= T * ROW
            return lent[:, a:spot[0]].rearrange("p (b n) -> p b n", b=n)

        xs = lend(2 * ST, ROW).rearrange("p (b t) c -> p b t c", b=2)
        hbuf, zs, b2s, ro, xb = lend(NH, HW), lend(ST - GA, D), lend(2, D), lend(NRO, D), lend(2, D)

        def cut_r(t, a, n):
            return t[:, a:a + n].rearrange("p (k n) -> p k n", k=KD)

        wah, wal = (w[:, 1, :].rearrange("p (k m d) -> p k m d", k=KD, m=4) for w in (w1h, w1l))

        zh = [cut_r(hi_part, b * KD * CW, KD * CW) for b in range(2)]
        zl = [cut_r(lo_part, b * KD * CW, KD * CW) for b in range(2)]
        oh, ol = cut_r(hi_part, 2 * KD * CW, KD * CW), cut_r(lo_part, 2 * KD * CW, KD * CW)
        eh, el = cut_r(hi_part, 3 * KD * CW, KD * CW), cut_r(lo_part, 3 * KD * CW, KD * CW)
        hh = hi_part[:].rearrange("p (f n) -> p f n", f=FB)
        hl = lo_part[:].rearrange("p (f n) -> p f n", f=FB)
        logits = bank[7][:, 0:TC * E].rearrange("p (t e) -> p t e", t=TC)
        ranks_ps = bank[5][:, 0:TC * E].rearrange("p (t e) -> p t e", t=TC)
        total_ps = bank[5][:, TC * E:TC * E + E]

        s_x = [sem(f"s_x{c}") for c in range(C)]
        s_small = sem("s_small")
        s_wa = sem("s_wa")
        s_shape = sem("s_shape")
        s_const = sem("s_const")
        s_conv = sem("s_conv")
        s_zero = sem("s_zero")
        s_init = sem("s_init")
        s_wah, s_wal = sem("s_wah"), sem("s_wal")
        r_st, r_ag, r_ve, r_rs, r_nb, r_z = (sem(f"r_{n}") for n in ("st", "ag", "ve", "rs", "nb", "z"))
        a_st, a_ag, a_ve, a_rs, a_z = (sem(f"a_{n}") for n in ("st", "ag", "ve", "rs", "z"))
        r_t, r_tc, r_lg = sem("r_t"), sem("r_tc"), sem("r_lg")
        rt_pick, rt_slot, rt_exp, rt_cnt, rt_used = (
            sem(f"rt_{n}") for n in ("pick", "slot", "exp", "cnt", "used"))
        s_disp = sem("s_disp")
        a_t, a_zh, a_zl, a_bo = sem("a_t"), sem("a_zh"), sem("a_zl"), sem("a_bo")
        a_qkv, a_ev, a_pair, a_exp = (sem(f"a_{n}") for n in ("qkv", "ev", "pair", "exp"))
        a_eh, a_el = sem("a_eh"), sem("a_el")
        a_cf, a_o, a_oh, a_ol, a_y, a_x2 = (sem(f"a_{n}") for n in ("cf", "o", "oh", "ol", "y", "x2"))
        s_x2st = sem("s_x2st")
        e_raw1, e_raw2 = sem("e_raw1"), sem("e_raw2")
        e_w1h, e_w1l, e_w2h, e_w2l = sem("e_w1h"), sem("e_w1l"), sem("e_w2h"), sem("e_w2l")
        e_xa, e_xs, e_b1, e_b2 = ([sem(f"e_{n}0"), sem(f"e_{n}1")] for n in ("xa", "xs", "b1", "b2"))
        e_z, e_tz, e_zh, e_zl = (sem(f"e_{n}") for n in ("z", "tz", "zh", "zl"))
        e_l1, e_g, e_hh, e_hl = sem("e_l1"), sem("e_g"), sem("e_hh"), sem("e_hl")
        e_y, e_xb, e_ro, e_idx = sem("e_y"), sem("e_xb"), sem("e_ro"), sem("e_idx")
        e_yt = [sem(f"e_yt{j}") for j in range(SURE, ST)]
        e_out, e_free = [sem(f"e_out{i}") for i in range(NRO)], sem("e_free")

        x_rows = x.rearrange("(p t) d -> p t d", p=P)
        x1_rows = x1.rearrange("(p t) d -> p t d", p=P)
        out_rows = out.rearrange("(p t) d -> p t d", p=P)

        def after(e, s, n):
            if n > 0:
                e.wait_ge(s, n)

        def credit(e, *sems):
            for s, n in sems:
                e.sem_inc(s, EC * n)

        block = ctx.enter_context(nc.Block())

        @block.sync
        def _(sp):
            def tiles(c):
                return slice(TC * c, TC * c + TC)

            for c in range(C):
                sp.dma_start(xe[:, tiles(c), 0:D], x_rows[:, tiles(c)]).then_inc(s_x[c], 16)
                if c == 0:
                    for dst, src in ((wgs, wg), (bqs, bqkv)):
                        sp.dma_start(dst[:], src).then_inc(s_small, 16)
                    sp.dma_start(bos[:], bo.partition_broadcast(P)[:, 0, :]).then_inc(s_small, 16)
            sp.wait_ge(s_const, 1)
            sp.dma_start(slots.rearrange("(p a) c -> p a c", p=ZP),
                         zero_row[0:ZP, None, :].broadcast_to([ZP, E * SL // ZP, ROW])).then_inc(s_zero, 16)

            def weights1(x):
                sp.wait_ge(e_w1l, KD * x.g)
                sp.dma_start(raw1[:], w12[bass.ds(x.e * P, P), 0:KD * F]).then_inc(e_raw1, 16)

            def weights2(x):
                sp.wait_ge(e_w2l, KD * x.g)
                sp.dma_start(raw2[:], w12[bass.ds(x.e * P, P), KD * F:]).then_inc(e_raw2, 16)

            def rows_of(x):
                sp.wait_ge(e_ro, NY * (x.g - 1))
                for t0, t1, done in ((0, GA, e_xa), (GA, ST - 1, e_xs)):
                    sp.dma_start(xs[:, x.b, t0:t1, :], slots[bass.ds(x.e * SL + t0 * P, (t1 - t0) * P)].rearrange(
                        "(j p) c -> p j c", p=P)).then_inc(done[x.b], 16)
                sp.dma_start(xs[0:TAIL, x.b, ST - 1, :],
                             slots[bass.ds(x.e * SL + (ST - 1) * P, TAIL)]).then_inc(e_xs[x.b], 16)
                sp.dma_start(b1s[:, x.b, :], b1[bass.ds(x.e * P, P)]).then_inc(e_b1[x.b], 16)
                sp.dma_start(b2s[:, x.b, :], b2[bass.ds(x.e, 1)].partition_broadcast(P)[:, 0, :]).then_inc(e_b2[x.b], 16)

            weights1(Turn(0, 0, 0))
            weights2(Turn(0, 0, 0))
            for c in range(C):
                sp.wait_ge(s_x[c], 16)
                sp.dma_start(x1_rows[:, tiles(c)], xe[:, tiles(c), 0:D]).then_inc(s_init, 16)
            for ffn in range(2):
                sp.wait_ge(s_disp, 16 * T * (ffn + 1))
                sp.wait_ge((s_init, s_x2st)[ffn], 16 * C)
                sp.wait_ge(rt_used, 5 * (ffn + 1))
                rows_of(Turn(ffn, 0, 0))
                rows_of(Turn(ffn, 0, 1))
                if ffn == 0:
                    weights1(Turn(0, 0, 1))
                weights2(Turn(ffn, 0, 1))
                with sp.Fori(0, E // 2 - 1) as i:
                    for b in range(2):
                        x = Turn(ffn, i + 1, b)
                        weights1(x)
                        weights2(x)
                        rows_of(x)
                if ffn == 0:
                    weights1(Turn(1, 0, 0))
                    weights2(Turn(1, 0, 0))
                    sp.wait_ge(e_w1l, KD * (Turn(1, 0, 0).g + 1))
                    sp.dma_start(raw1[:], wa).then_inc(s_wa, 16)
                    for i in range(NRO):
                        sp.wait_ge(e_out[i], 16 * E * (NY // NRO))
                    for c in range(C):
                        sp.dma_start(xe[:, tiles(c), 0:D], x1_rows[:, tiles(c)]).then_inc(s_x[c], 16)
                    sp.wait_ge(s_wal, 1)
                    weights1(Turn(1, 0, 1))
                    for c in range(C):
                        sp.wait_ge(a_x2, 2 * (c + 1))
                        sp.dma_start(out_rows[:, tiles(c)], xe[:, tiles(c), 0:D]).then_inc(s_x2st, 16)
            for i in range(NRO):
                sp.wait_ge(e_out[i], 16 * 2 * E * (NY // NRO))

        @block.gpsimd
        def _(pool):
            g_ = nc.gpsimd
            credit(pool, (e_free, NY))
            g_.memset(zero_row[:], 0.0).then_inc(s_const, 1)
            g_.memset(ident[:], 0.0)
            g_.memset(ones_f[:], 1.0)
            g_.memset(upto_f[:], 1.0)
            g_.memset(head_f[:], 1.0)
            g_.memset(half[:], -0.5)
            g_.memset(base[:], 0.0)
            g_.iota(tok_i[:], pattern=[[1, T]], base=0, channel_multiplier=T)
            g_.iota(pos_i[:], pattern=[[P, ST]], base=0, channel_multiplier=1)
            g_.iota(code_i[:], pattern=[[-1, E]], base=E, channel_multiplier=0).then_inc(s_shape, 1)
            pool.wait_ge(s_shape, 1)
            g_.affine_select(out=ident[:], in_=ident[:], compare_op=ALU.not_equal, fill=1.0, base=0,
                             pattern=[[-1, P]], channel_multiplier=1)
            g_.affine_select(out=upto_f[:], in_=upto_f[:], compare_op=ALU.is_ge, fill=0.0, base=0,
                             pattern=[[1, P]], channel_multiplier=-1)
            blk = head_f[:].rearrange("p (h d) -> p h d", d=HD)
            g_.affine_select(out=blk, in_=blk, compare_op=ALU.is_ge, fill=0.0, base=0,
                             pattern=[[-HD, P // HD], [0, HD]], channel_multiplier=1).then_inc(s_shape, 1)
            pool.wait_ge(s_shape, 2)
            g_.affine_select(out=blk, in_=blk, compare_op=ALU.is_ge, fill=0.0, base=HD - 1,
                             pattern=[[HD, P // HD], [0, HD]], channel_multiplier=-1).then_inc(s_const, 1)

            def rstd(ve, rs, c, n):
                pool.wait_ge(ve, n + 1)
                v = xe[:, TC * c:TC * c + TC, RSTD]
                g_.tensor_tensor(v, v, half[:], ALU.pow).then_inc(rs, 1)

            def dispatch(c, n):
                pool.wait_ge(rt_slot, SLOT * (n + 1))
                if n == 0:
                    pool.wait_ge(s_zero, 16)
                for t in range(TC * c, TC * c + TC):
                    g_.indirect_dma_start(out=slots, out_offset=bass.IndirectOffsetOnAxis(ap=slot_i[:, t:t + 1], axis=0),
                                          in_=xe[:, t, :], in_offset=None, bounds_check=E * SL - 1,
                                          oob_is_err=False).then_inc(s_disp, 16)

            def scattered(y):
                pool.wait_ge(e_out[y % NRO], 16 * (y // NRO + 1))
                pool.sem_inc(e_free, 1)

            def scatter(ffn, y):
                j = y % NY
                rows = P if j < ST - 1 else TAIL
                pool.wait_ge(e_ro, EC * NY + y + 1)
                g_.indirect_dma_start(out=(x1, out)[ffn], out_offset=bass.IndirectOffsetOnAxis(
                    ap=tok_idx[0:rows, y // NY % 2, j:j + 1], axis=0), in_=ro[0:rows, y % NRO, :], in_offset=None,
                    bounds_check=N - 1, oob_is_err=False).then_inc(e_out[y % NRO], 16)

            def results(ffn):
                pool.wait_ge((s_init, s_x2st)[ffn], 16 * C)
                first, end = NY * E * ffn, NY * E * (ffn + 1)
                for y in range(first, end + 2):
                    if y < end:
                        if y % NY == 0:
                            pool.wait_ge(e_idx, 2 * (y // NY + EC + 1))
                        scatter(ffn, y)
                    if y >= first + 2:
                        scattered(y - 2)

            for c in range(C):
                rstd(r_ve, r_rs, c, c)
                if c >= AHEAD:
                    dispatch(c - AHEAD, c - AHEAD)
            for c in range(C - AHEAD, C):
                dispatch(c, c)
            results(0)

            def add_bo(c):
                pool.wait_ge(a_z, c + 1)
                rows = xe[:, TC * c:TC * c + TC, 0:D]
                g_.tensor_tensor(rows, rows, bos[:].unsqueeze(1).broadcast_to([P, TC, D]), ALU.add).then_inc(a_bo, 1)

            def pair(c, m):
                pool.wait_ge(a_ev, 6 * c + 2 * m + 2)
                g_.tensor_tensor(sqq[:, m, :], sqq[:, m, :], sqk[:, m, :], ALU.add).then_inc(a_pair, 1)

            for s in range(-2, C + 4):
                if 0 <= s + 1 < C:
                    add_bo(s + 1)
                if 0 <= s < C:
                    pair(s, 0)
                if 0 <= s - 3 < C and s >= C:
                    dispatch(s - 3, C + s - 3)
                if 0 <= s < C:
                    pair(s, 1)
                if 0 <= s + 2 < C:
                    rstd(a_ve, a_rs, s + 2, s + 2)
                if 0 <= s - 3 < C and s < C:
                    dispatch(s - 3, C + s - 3)
                if 0 <= s - 1 < C:
                    rstd(r_ve, r_rs, s - 1, C + s - 1)
            results(1)

        @block.scalar
        def _(act):
            s_ = nc.scalar

            def router_copy(c, ffn):
                n = C * ffn + c
                for k in range(KD):
                    act.wait_ge(r_t, KD * n + k + 1)
                    after(act, r_lg, n)
                    s_.copy(zrt[:, k, :], bank[k][:]).then_inc(r_tc, 1)

            def router_exp(n):
                act.wait_ge(rt_pick, PICK * n + 3)
                s_.activation(dlt[:], dlt[:], ACT.Exp).then_inc(rt_exp, 1)

            def router_norm(c, n):
                act.wait_ge(r_nb, n + 1)
                after(act, r_t, KD * n)
                for i in range(TC):
                    t = TC * c + i
                    q = s_.activation(zr[:, i, :], xe[:, t, 0:D], ACT.Identity, bias=nbias[:, n % 2, i:i + 1],
                                      scale=xe[:, t, RSTD:RSTD + 1])
                q.then_inc(r_z, 1)

            def gelu(x, gi, fs, end=GA * P):
                c0, c1, t1 = GROUPS[gi][0], end, GROUPS[gi][3]
                for f in fs:
                    i = FB * gi + f
                    u = HU * x.g + i
                    h = hbuf[:, i % NH, 0:c1 - c0]
                    act.wait_ge(e_l1, u + 1)
                    act.wait_ge(e_hl, u + 1 - NH)
                    s_.activation(h, bank[2 + i % 4][:, 0:c1 - c0], ACT.Gelu, bias=b1s[:, x.b, f:f + 1]).then_inc(e_g, 1)
                    act.wait_ge(e_g, u + 1)
                    act.wait_ge(e_y, SURE * (x.g - 1) + min(t1, SURE))
                    if gi == 1 and f == 0:
                        for q in e_yt:
                            act.wait_ge(q, x.g)
                    s_.copy(hh[:, f, c0:c1], h).then_inc(e_hh, 1)

            def slots_hi(x, gi):
                c0, c1, t0, t1 = GROUPS[gi]
                act.wait_ge(e_tz, ST * x.g + t1)
                act.wait_ge(e_l1, HU * (x.g - 1) + FB * (gi + 1))
                for k in range(KD):
                    s_.copy(zth[:, k, c0:c1], bank[k][:, 0:c1 - c0]).then_inc(e_zh, 1)

            def w1_hi(x, k):
                act.wait_ge(e_raw1, 16 * (x.g - EC + 1))
                act.wait_ge(e_l1, HU * (x.g - 1))
                ks = slice(k * F, (k + 1) * F)
                s_.copy(w1h[:, x.b, ks], raw1[:, ks]).then_inc(e_w1h, 1)

            def w2_hi(x, k):
                act.wait_ge(e_raw2, 16 * (x.g - EC + 1))
                act.wait_ge(e_y, SURE * (x.g - 1))
                if k == 0:
                    for q in e_yt:
                        act.wait_ge(q, x.g - 1)
                ks = slice(k * FB * D // 2, (k + 1) * FB * D // 2)
                s_.copy(w2h[:, x.b, ks], raw2[:, ks]).then_inc(e_w2h, 1)

            credit(act, (e_g, HU), (e_hh, HU), (e_zh, 2 * KD), (e_w1h, KD), (e_w2h, KD))
            act.wait_ge(s_small, 48)
            for c in range(C + 1):
                if c < C:
                    router_norm(c, c)
                if c >= 1:
                    router_exp(c - 1)
                if c < C:
                    router_copy(c, 0)
            for k in range(KD):
                w1_hi(Turn(0, 0, 0), k)
            for k in range(KD):
                w2_hi(Turn(0, 0, 0), k)
            for ffn in range(2):
                first = Turn(ffn, 0, 0)
                s_.activation(spare[:], bqs[:, 0, 0:1], ACT.Gelu)
                act.wait_ge(e_b1[0], 16 * (first.n + 1))
                if ffn == 1:
                    act.wait_ge(a_y, 2 * C)
                slots_hi(first, 0)
                gelu(first, 0, range(0, 3))
                slots_hi(first, 1)
                gelu(first, 0, range(3, 8))
                act.wait_ge(rt_used, 5 * (ffn + 1))
                for x, y, last in turns(ffn, act):
                    split = not (last and ffn == 1)
                    count = act.value_load(filled[0:1, bass.ds(x.e, 1)])
                    if split and not last:
                        w1_hi(y, 0)
                    second(act, count, gelu, x, range(0, 4))
                    if split and not last:
                        w1_hi(y, 1)
                    second(act, count, gelu, x, range(4, 6))
                    if last:
                        second(act, count, gelu, x, range(6, 8))
                    else:
                        slots_hi(y, 0)
                    if split and last:
                        w1_hi(y, 0)
                        w1_hi(y, 1)
                    if split:
                        w2_hi(y, 0)
                    if not last:
                        second(act, count, gelu, x, range(6, 8))
                    if not last:
                        act.wait_ge(e_b1[y.b], 16 * (y.n + 1))
                        gelu(y, 0, range(0, 3))
                    if split:
                        w2_hi(y, 1)
                    if not last:
                        slots_hi(y, 1)
                        gelu(y, 0, range(3, 8))
                if ffn == 1:
                    break

                s_.activation(spare[:], bqs[:, 0, 0:1], ACT.Exp)
                act.wait_ge(s_wa, 16)
                act.wait_ge(e_l1, HU * (E + EC))
                s_.copy(w1h[:, 1, :], raw1[:]).then_inc(s_wah, 1)

                def z_hi(c):
                    for k in range(KD):
                        act.wait_ge(a_t, KD * c + k + 1)
                        after(act, a_qkv, 6 * (c - 1))
                        s_.copy(zh[c % 2][:, k, :], bank[k][:]).then_inc(a_zh, 1)

                def o_hi(c, m):
                    act.wait_ge(a_o, KD * c + m + 1)
                    after(act, a_y, 2 * c)
                    s_.copy(oh[:, m, :], ob[:, m, :]).then_inc(a_oh, 1)

                def squares(c, m, parts=(0, 1)):
                    for i in parts:
                        sq, which = ((sqq, 0), (sqk, 1))[i]
                        u = 6 * c + 2 * m + i
                        act.wait_ge(a_qkv, u + 1)
                        after(act, a_cf, KD * (c - 1) + m + 1)
                        s_.activation(sq[:, m, :], bank[2 + u % 3][:], ACT.Square,
                                      bias=bqs[:, which, m:m + 1]).then_inc(a_ev, 1)

                def head_exp(c, m):
                    act.wait_ge(a_pair, KD * c + m + 1)
                    s_.activation(sqq[:, m, :], sqq[:, m, :], ACT.Exp, scale=-0.5).then_inc(a_exp, 1)
                    act.wait_ge(a_exp, KD * c + m + 1)
                    after(act, a_cf, KD * (c - 1) + m + 1)
                    s_.copy(eh[:, m, :], sqq[:, m, :]).then_inc(a_eh, 1)

                def values(c):
                    for m in range(KD):
                        u = 6 * c + 4 + m
                        act.wait_ge(a_qkv, u + 1)
                        after(act, a_o, KD * c)
                        s_.activation(vb[:, m, :], bank[2 + u % 3][:], ACT.Identity,
                                      bias=bqs[:, 2, m:m + 1]).then_inc(a_ev, 1)

                for s in range(-1, C + 4):
                    now, prev = 0 <= s < C, 0 <= s - 1 < C
                    if 0 <= s - 2 < C:
                        router_norm(s - 2, C + s - 2)
                    if prev:
                        o_hi(s - 1, 0)
                    if now:
                        squares(s, 0)
                    if 0 <= s - 3 < C:
                        router_exp(C + s - 3)
                    if now:
                        squares(s, 1, (0,))
                    if prev:
                        o_hi(s - 1, 1)
                    if 0 <= s + 1 < C:
                        z_hi(s + 1)
                    if now:
                        head_exp(s, 0)
                        squares(s, 1, (1,))
                        values(s)
                        head_exp(s, 1)
                    if 0 <= s - 2 < C:
                        router_copy(s - 2, 1)

        @block.vector
        def _(dve):
            v_ = nc.vector

            def tile_stats(c, n, st, par, i):
                v_.bn_stats(stats[:, par, i, :], xe[:, TC * c + i, 0:D]).then_inc(st, 1)

            def ln_moments(c, n, st, ag, ve, par):
                for i in range(TC):
                    dve.wait_ge(st, TC * n + i + 1)
                    v_.bn_aggr(xe[:, TC * c + i, MEAN:RSTD + 1], stats[:, par, i, :]).then_inc(ag, 1)
                dve.wait_ge(ag, TC * (n + 1))
                v = xe[:, TC * c:TC * c + TC, RSTD]
                v_.tensor_scalar(v, v, EPS, None, ALU.add).then_inc(ve, 1)

            def router_bias(c, n):
                dve.wait_ge(r_rs, n + 1)
                v_.scalar_tensor_tensor(out=nbias[:, n % 2, :], in0=xe[:, TC * c:TC * c + TC, MEAN], scalar=-1.0,
                                        in1=xe[:, TC * c:TC * c + TC, RSTD], op0=ALU.mult,
                                        op1=ALU.mult).then_inc(r_nb, 1)

            def ln_norm(c, n, rs, z, zdone):
                dve.wait_ge(rs, n + 1)
                for i in range(TC):
                    t = TC * c + i
                    q = v_.tensor_scalar(z[:, i, :], xe[:, t, 0:D], xe[:, t, MEAN:MEAN + 1],
                                         xe[:, t, RSTD:RSTD + 1], ALU.subtract, ALU.mult)
                q.then_inc(zdone, 1)

            def pick(n, i):
                if i == 0:
                    dve.wait_ge(r_lg, n + 1)
                    q = v_.tensor_reduce(col[:, 0, :], logits, AX.X, ALU.max)
                else:
                    dve.wait_ge(rt_pick, PICK * n + i)
                if i == 1:
                    q = v_.tensor_tensor(dlt[:], logits, col[:, 0, :].unsqueeze(2).broadcast_to([P, TC, E]),
                                         ALU.subtract)
                elif i == 2:
                    q = v_.scalar_tensor_tensor(out=code[:], in0=dlt[:], scalar=0.0,
                                                in1=first_code[:].unsqueeze(1).broadcast_to([P, TC, E]),
                                                op0=ALU.is_ge, op1=ALU.mult)
                elif i == 3:
                    q = v_.tensor_reduce(col[:, 1, :], code[:], AX.X, ALU.max)
                elif i == 4:
                    q = v_.tensor_tensor(hot[:], code[:], col[:, 1, :].unsqueeze(2).broadcast_to([P, TC, E]),
                                         ALU.is_equal)
                elif i == 5:
                    dve.wait_ge(rt_exp, n + 1)
                    q = v_.tensor_reduce(col[:, 2, :], dlt[:], AX.X, ALU.add)
                elif i == 6:
                    q = v_.reciprocal(col[:, 3, :], col[:, 2, :])
                q.then_inc(rt_pick, 1)

            def slot(c, n, i):
                tiles = slice(TC * c, TC * c + TC)
                if i == 0:
                    dve.wait_ge(rt_pick, PICK * (n + 1))
                    q = v_.tensor_scalar(xe[:, tiles, WGT], col[:, 3, :], 0.5, None, ALU.mult)
                elif i == 1:
                    dve.wait_ge(rt_cnt, n + 1)
                    q = v_.tensor_tensor(ranks[:], ranks_ps, base[:].unsqueeze(1).broadcast_to([P, TC, E]), ALU.add)
                elif i == 2:
                    q = v_.tensor_scalar(col[:, 4, :], col[:, 1, :], -float(SL), float(E * SL - 1), ALU.mult, ALU.add)
                elif i == 3:
                    dve.wait_ge(rt_slot, SLOT * n + 2)
                    q = v_.tensor_tensor(base[:], base[:], total_ps, ALU.add)
                elif i == 4:
                    q = v_.tensor_tensor(ranks[:], ranks[:], hot[:], ALU.mult)
                elif i == 5:
                    dve.wait_ge(rt_slot, SLOT * n + 5)
                    q = v_.tensor_reduce(col[:, 5, :], ranks[:], AX.X, ALU.add)
                elif i == 6:
                    dve.wait_ge(rt_slot, SLOT * n + 6)
                    q = v_.tensor_scalar(col[:, 6, :], col[:, 5, :], float(CAP), FAR, ALU.is_gt, ALU.mult)
                elif i == 7:
                    q = v_.tensor_tensor(col[:, 7, :], col[:, 5, :], col[:, 4, :], ALU.add)
                elif i == 8:
                    dve.wait_ge(rt_slot, SLOT * n + 8)
                    q = v_.tensor_tensor(slot_i[:, tiles], col[:, 7, :], col[:, 6, :], ALU.add)
                elif i == 9:
                    q = v_.tensor_copy(xe[:, tiles, TOK], tok_i[:, tiles])
                q.then_inc(rt_slot, 1)

            def route_end(ffn):
                dve.wait_ge(rt_slot, SLOT * C * (ffn + 1))
                v_.tensor_scalar(col[:].rearrange("p a b -> p (a b)")[:, 0:E], base[:], float(CAP), None,
                                 ALU.min).then_inc(rt_used, 1)
                dve.wait_ge(rt_used, 5 * ffn + 1)
                v_.tensor_tensor(unused[:], slot_pos[:].unsqueeze(1).broadcast_to([P, E, ST]),
                                 col[:].rearrange("p a b -> p (a b)")[:, 0:E].unsqueeze(2).broadcast_to([P, E, ST]),
                                 ALU.is_ge).then_inc(rt_used, 1)
                dve.wait_ge(rt_used, 5 * ffn + 2)
                v_.tensor_scalar(unused[:], unused[:], FAR, None, ALU.mult).then_inc(rt_used, 1)
                v_.tensor_copy(filled[:], col[:].rearrange("p a b -> p (a b)")[:, 0:E]).then_inc(rt_used, 1)
                v_.memset(base[:], 0.0).then_inc(rt_used, 1)

            def w1_lo(x, k):
                dve.wait_ge(e_w1h, KD * x.g + k + 1)
                ks = slice(k * F, (k + 1) * F)
                v_.tensor_tensor(w1l[:, x.b, ks], raw1[:, ks], w1h[:, x.b, ks].bitcast(F32),
                                 ALU.subtract).then_inc(e_w1l, 1)

            def w2_lo(x, k):
                dve.wait_ge(e_w2h, KD * x.g + k + 1)
                ks = slice(k * FB * D // 2, (k + 1) * FB * D // 2)
                v_.tensor_tensor(w2l[:, x.b, ks], raw2[:, ks], w2h[:, x.b, ks].bitcast(F32),
                                 ALU.subtract).then_inc(e_w2l, 1)

            def slots_z(x, gi):
                b, (c0, c1, t0, t1) = x.b, GROUPS[gi]
                if gi == 0:
                    dve.wait_ge(e_xa[b], 16 * (x.n + 1))
                else:
                    dve.wait_ge(e_xs[b], 32 * (x.n + 1))
                dve.wait_ge(e_tz, ST * x.g + t0)
                for j in range(t0, t1):
                    rows = P if j < ST - 1 else TAIL
                    v_.tensor_scalar(zs[0:rows, j - t0, :], xs[0:rows, b, j, 0:D], xs[0:rows, b, j, MEAN:MEAN + 1],
                                     xs[0:rows, b, j, RSTD:RSTD + 1], ALU.subtract, ALU.mult).then_inc(e_z, 1)

            def slots_lo(x, gi):
                c0, c1, t0, t1 = GROUPS[gi]
                for k in range(KD):
                    dve.wait_ge(e_zh, (2 * x.g + gi) * KD + k + 1)
                    v_.tensor_tensor(ztl[:, k, c0:c1], bank[k][:, 0:c1 - c0], zth[:, k, c0:c1].bitcast(F32),
                                     ALU.subtract).then_inc(e_zl, 1)

            def goals(x):
                dve.wait_ge(e_free, NY * (x.g - 1))
                v_.tensor_tensor(tok_idx[:, x.b, 0:ST - 1], xs[:, x.b, 0:ST - 1, TOK],
                                 unused[:, bass.ds(x.e, 1), 0:ST - 1].squeeze(1), ALU.add).then_inc(e_idx, 1)
                v_.tensor_tensor(tok_idx[0:TAIL, x.b, ST - 1:ST], xs[0:TAIL, x.b, ST - 1, TOK:TOK + 1],
                                 unused[0:TAIL, bass.ds(x.e, 1), ST - 1:ST].squeeze(1), ALU.add).then_inc(e_idx, 1)

            def hidden(x, gi, fs, end=GA * P):
                c0, c1, t1 = GROUPS[gi][0], end, GROUPS[gi][3]
                for f in fs:
                    i = FB * gi + f
                    dve.wait_ge(e_hh, HU * x.g + i + 1)
                    v_.tensor_tensor(hl[:, f, c0:c1], hbuf[:, i % NH, 0:c1 - c0], hh[:, f, c0:c1].bitcast(F32),
                                     ALU.subtract).then_inc(e_hl, 1)

            def result(x, j):
                yy = NY * x.g + j
                rows = P if j < ST - 1 else TAIL
                w = xs[0:rows, x.b, j, WGT:WGT + 1]
                if j == 0:
                    dve.wait_ge(e_b2[x.b], 16 * (x.n + 1))
                v_.scalar_tensor_tensor(out=xb[0:rows, j % 2, :], in0=b2s[0:rows, x.b, :], scalar=w,
                                        in1=xs[0:rows, x.b, j, 0:D], op0=ALU.mult, op1=ALU.add).then_inc(e_xb, 1)
                dve.wait_ge(e_xb, yy + 1)
                dve.wait_ge(e_free, yy + 1 - NRO)
                if j < SURE:
                    dve.wait_ge(e_y, SURE * x.g + j + 1)
                else:
                    dve.wait_ge(e_yt[j - SURE], x.g + 1)
                v_.scalar_tensor_tensor(out=ro[0:rows, j % NRO, :], in0=bank[6 + j % 2][0:rows, 0:D], scalar=w,
                                        in1=xb[0:rows, j % 2, :], op0=ALU.mult, op1=ALU.add).then_inc(e_ro, 1)

            def result_tail(x, count, j):
                with dve.If(count > j * P):
                    result(x, j)
                    if j + 1 < ST:
                        result_tail(x, count, j + 1)
                with dve.Else():
                    dve.wait_ge(e_ro, NY * x.g + j)
                    for _ in range(j, ST):
                        dve.sem_inc(e_xb, 1)
                        dve.sem_inc(e_ro, 1)

            credit(dve, (e_w1l, KD), (e_w2l, KD), (e_z, ST), (e_zl, 2 * KD), (e_idx, 2), (e_hl, HU), (e_xb, NY),
                   (e_ro, NY))
            dve.wait_ge(s_const, 2)
            v_.tensor_copy(upto[:], upto_f[:])
            v_.tensor_copy(ones[:], ones_f[:])
            v_.tensor_copy(head_r[:], head_f[:])
            v_.tensor_copy(slot_pos[:], pos_i[:])
            v_.tensor_copy(first_code[:], code_i[:]).then_inc(s_conv, 1)
            dve.wait_ge(s_conv, 1)
            for s in range(-1, C + 2):
                new, old = 0 <= s + 1 < C, 0 <= s - 1 < C
                if new:
                    dve.wait_ge(s_x[s + 1], 16)
                for i in range(4):
                    if new:
                        tile_stats(s + 1, s + 1, r_st, 0, i)
                if new:
                    ln_moments(s + 1, s + 1, r_st, r_ag, r_ve, 0)
                if old:
                    for i in range(PICK):
                        pick(s - 1, i)
                if new:
                    router_bias(s + 1, s + 1)
                if old:
                    for i in range(SLOT):
                        slot(s - 1, s - 1, i)
            for k in range(KD):
                w1_lo(Turn(0, 0, 0), k)
            for k in range(KD):
                w2_lo(Turn(0, 0, 0), k)
            for ffn in range(2):
                route_end(ffn)
                first = Turn(ffn, 0, 0)
                slots_z(first, 0)
                slots_lo(first, 0)
                slots_z(first, 1)
                goals(first)
                hidden(first, 0, range(0, 3))
                slots_lo(first, 1)
                hidden(first, 0, range(3, 8))
                dve.wait_ge(rt_used, 5 * (ffn + 1))
                for x, y, last in turns(ffn, dve):
                    split = not (last and ffn == 1)
                    count = dve.value_load(filled[0:1, bass.ds(x.e, 1)])
                    second(dve, count, hidden, x, range(0, 4))
                    if last:
                        result(x, 0)
                        second(dve, count, hidden, x, range(4, 6))
                        second(dve, count, hidden, x, range(6, 8))
                        result(x, 1)
                        if split:
                            w1_lo(y, 0)
                        result(x, 2)
                        if split:
                            w1_lo(y, 1)
                        result(x, 3)
                        result_tail(x, count, SURE)
                        if split:
                            w2_lo(y, 0)
                            w2_lo(y, 1)
                        continue
                    slots_z(y, 0)
                    w1_lo(y, 0)
                    result(x, 0)
                    second(dve, count, hidden, x, range(4, 6))
                    slots_lo(y, 0)
                    w1_lo(y, 1)
                    result(x, 1)
                    second(dve, count, hidden, x, range(6, 8))
                    slots_z(y, 1)
                    w2_lo(y, 0)
                    hidden(y, 0, range(0, 3))
                    result(x, 2)
                    w2_lo(y, 1)
                    slots_lo(y, 1)
                    hidden(y, 0, range(3, 6))
                    result(x, 3)
                    hidden(y, 0, range(6, 8))
                    goals(y)
                    result_tail(x, count, SURE)
                if ffn == 1:
                    break

                dve.wait_ge(s_wah, 1)
                v_.tensor_tensor(w1l[:, 1, :], raw1[:], w1h[:, 1, :].bitcast(F32), ALU.subtract).then_inc(s_wal, 1)

                def z_lo(c):
                    for m in range(KD):
                        dve.wait_ge(a_zh, KD * c + m + 1)
                        v_.tensor_tensor(zl[c % 2][:, m, :], bank[m][:], zh[c % 2][:, m, :].bitcast(F32),
                                         ALU.subtract).then_inc(a_zl, 1)

                def weigh(c, m):
                    dve.wait_ge(a_cf, KD * c + m + 1)
                    dve.wait_ge(a_ev, 6 * c + 5 + m)
                    after(dve, a_ol, KD * (c - 1) + m + 1)
                    after(dve, a_oh, KD * (c - 1) + m + 1)
                    v_.tensor_tensor(ob[:, m, :], bank[5][:], vb[:, m, :], ALU.mult).then_inc(a_o, 1)

                def e_lo(c, m):
                    dve.wait_ge(a_eh, KD * c + m + 1)
                    v_.tensor_tensor(el[:, m, :], sqq[:, m, :], eh[:, m, :].bitcast(F32),
                                     ALU.subtract).then_inc(a_el, 1)

                def o_lo(c, m):
                    dve.wait_ge(a_oh, KD * c + m + 1)
                    v_.tensor_tensor(ol[:, m, :], ob[:, m, :], oh[:, m, :].bitcast(F32),
                                     ALU.subtract).then_inc(a_ol, 1)

                def add_y(c, h):
                    dve.wait_ge(a_bo, c + 1)
                    h += 2 * c
                    dve.wait_ge(a_y, h + 1)
                    xt = xe[:, 2 * h:2 * h + 2, 0:D]
                    v_.tensor_tensor(xt, bank[6][:].rearrange("p (t d) -> p t d", t=2), xt,
                                     ALU.add).then_inc(a_x2, 1)

                for s in range(-2, C + 4):
                    now, prev = 0 <= s < C, 0 <= s - 1 < C
                    new, old = 0 <= s + 2 < C, 0 <= s - 3 < C
                    n = C + s - 3

                    def a_stats(i):
                        if new:
                            tile_stats(s + 2, s + 2, a_st, 1, i)

                    if new:
                        dve.wait_ge(s_x[s + 2], 32)
                    if prev:
                        e_lo(s - 1, 1)
                        weigh(s - 1, 0)
                    if old:
                        pick(n, 0)
                    a_stats(0)
                    if old:
                        pick(n, 1)
                    a_stats(1)
                    if old:
                        pick(n, 2)
                    if prev:
                        o_lo(s - 1, 0)
                    if old:
                        pick(n, 3)
                    if prev:
                        weigh(s - 1, 1)
                    if old:
                        pick(n, 4)
                    a_stats(2)
                    a_stats(3)
                    if old:
                        pick(n, 5)
                    if prev:
                        o_lo(s - 1, 1)
                    if old:
                        pick(n, 6)
                    if new:
                        ln_moments(s + 2, s + 2, a_st, a_ag, a_ve, 1)
                    if 0 <= s + 1 < C:
                        z_lo(s + 1)
                    if now:
                        e_lo(s, 0)
                    if old:
                        for i in range(SLOT):
                            slot(s - 3, n, i)
                    for h in range(2):
                        if prev:
                            add_y(s - 1, h)
                            dve.wait_ge(a_x2, 2 * (s - 1) + h + 1)
                            for i in range(2):
                                tile_stats(s - 1, C + s - 1, r_st, 0, 2 * h + i)
                        if new and h == 0:
                            after(dve, a_t, KD * (s + 2))
                            ln_norm(s + 2, s + 2, a_rs, za, a_z)
                    if prev:
                        ln_moments(s - 1, C + s - 1, r_st, r_ag, r_ve, 0)
                        router_bias(s - 1, C + s - 1)

        @block.tensor
        def _(pe):
            t_ = nc.tensor

            def three(o, ah, al, bh, bl, first, last):
                t_.matmul(o, ah, bh, start=first, stop=False)
                t_.matmul(o, ah, bl, start=False, stop=False)
                return t_.matmul(o, al, bh, start=False, stop=last)

            def across(o, a, rows):
                return t_.transpose(o, a, ident[0:rows, 0:rows])

            def transpose_z(c, n, z, zdone, done):
                pe.wait_ge(zdone, n + 1)
                for k in range(KD):
                    for i in range(TC):
                        q = across(bank[k][:, i * P:(i + 1) * P], z[:, i, k * P:(k + 1) * P], P)
                    q.then_inc(done, 1)

            def router_logits(n):
                pe.wait_ge(r_tc, KD * (n + 1))
                after(pe, rt_pick, PICK * (n - 1) + 2)
                for i in range(TC):
                    for k in range(KD):
                        q = t_.matmul(logits[:, i, :], zrt[:, k, i * P:(i + 1) * P], wgs[:, k, :],
                                      start=(k == 0), stop=(k == KD - 1))
                q.then_inc(r_lg, 1)

            def counts(n):
                pe.wait_ge(rt_pick, PICK * n + 5)
                after(pe, rt_slot, SLOT * n)
                h = hot[:].rearrange("p t e -> p (t e)")
                w = TC * E
                t_.matmul(bank[5][:, 0:w], upto[:], h, start=True, stop=False)
                for i in range(1, TC):
                    t_.matmul(bank[5][:, E * i:w], ones[:], h[:, 0:w - E * i], start=False, stop=(i == TC - 1))
                for i in range(TC):
                    q = t_.matmul(total_ps, ones[:], h[:, E * i:E * (i + 1)], start=(i == 0), stop=(i == TC - 1))
                q.then_inc(rt_cnt, 1)

            def slots_t(x, gi, used=ST):
                c0, c1, t0, t1 = GROUPS[gi]
                pe.wait_ge(e_zl, KD * (2 * x.g + gi))
                for j in range(t0, min(t1, used)):
                    rows = P if j < ST - 1 else TAIL
                    if j < ST - 1:
                        pe.wait_ge(e_z, ST * x.g + j + (2 if j == ST - 2 else 1))
                    for k in range(KD):
                        q = across(bank[k][:, (j - t0) * P:(j - t0) * P + rows],
                                   zs[0:rows, j - t0, k * P:(k + 1) * P], rows)
                    q.then_inc(e_tz, 1 if j + 1 < min(t1, used) else t1 - j)

            def layer1(x, gi, fs, end=GA * P):
                c0, c1, t1 = GROUPS[gi][0], end, GROUPS[gi][3]
                pe.wait_ge(e_zl, KD * (2 * x.g + gi + 1))
                pe.wait_ge(e_w1l, KD * (x.g + 1))
                wh, wl = (w[:, x.b, :].rearrange("p (k f) -> p k f", k=KD) for w in (w1h, w1l))
                for f in fs:
                    i = FB * gi + f
                    pe.wait_ge(e_g, HU * x.g + i - 3)
                    o = bank[2 + i % 4][:, 0:c1 - c0]
                    for k in range(KD):
                        ks = slice(f * P, (f + 1) * P)
                        q = three(o, wh[:, k, ks], wl[:, k, ks], zth[:, k, c0:c1], ztl[:, k, c0:c1],
                                  k == 0, k == KD - 1)
                    q.then_inc(e_l1, 1)

            def warm_up(n, b):
                for _ in range(n):
                    t_.matmul(bank[b][:], w1h[:, 0, 0:P], w1h[:, 0, 0:512], start=True, stop=True)

            def layer2(x, j):
                gi = 0 if j < GA else 1
                yy = NY * x.g + j
                rows = P if j < ST - 1 else TAIL
                pe.wait_ge(e_hl, HU * x.g + FB * (gi + 1))
                pe.wait_ge(e_w2l, KD * (x.g + 1))
                pe.wait_ge(e_ro, yy - 1)
                o = bank[6 + j % 2][0:rows, 0:D]
                wh, wl = (w[:, x.b, :].rearrange("p (f d) -> p f d", f=FB) for w in (w2h, w2l))
                for f in range(FB):
                    ns = slice(j * P, j * P + rows)
                    q = three(o, hh[:, f, ns], hl[:, f, ns], wh[:, f, :], wl[:, f, :], f == 0, f == FB - 1)
                q.then_inc(e_y if j < SURE else e_yt[j - SURE], 1)

            def layer2_tail(x, count, j):
                with pe.If(count > j * P):
                    layer2(x, j)
                    if j + 1 < ST:
                        layer2_tail(x, count, j + 1)
                with pe.Else():
                    for q in e_yt[j - SURE:]:
                        pe.sem_inc(q, 1)

            credit(pe, (e_tz, ST), (e_l1, HU), (e_y, SURE), (e_yt[0], 1), (e_yt[1], 1))
            pe.wait_ge(s_const, 2)
            pe.wait_ge(s_small, 48)
            pe.wait_ge(s_conv, 1)
            for s in range(C + 1):
                if s < C:
                    after(pe, r_tc, KD * s)
                    transpose_z(s, s, zr, r_z, r_t)
                if s >= 1:
                    counts(s - 1)
                if s < C:
                    router_logits(s)
            for ffn in range(2):
                first = Turn(ffn, 0, 0)
                pe.wait_ge(e_w1l, KD * (first.g + 1))
                pe.wait_ge(s_disp, 16 * T * (ffn + 1))
                warm_up(WARM, 7)
                slots_t(first, 0)
                layer1(first, 0, range(0, 3))
                slots_t(first, 1)
                layer1(first, 0, range(3, 8))
                pe.wait_ge(rt_used, 5 * (ffn + 1))
                for x, y, last in turns(ffn, pe):
                    count = pe.value_load(filled[0:1, bass.ds(x.e, 1)]) if x.b == 0 else following
                    second(pe, count, layer1, x, range(0, 4))
                    layer2(x, 0)
                    second(pe, count, layer1, x, range(4, 6))
                    if last:
                        second(pe, count, layer1, x, range(6, 8))
                        layer2(x, 1)
                    else:
                        slots_t(y, 0)
                        layer2(x, 1)
                        second(pe, count, layer1, x, range(6, 8))
                        following = pe.value_load(filled[0:1, bass.ds(y.e, 1)])
                    if not last:
                        layer1(y, 0, range(0, 3))
                    layer2(x, 2)
                    if not last:
                        with pe.If(following > SURE * P):
                            slots_t(y, 1)
                        with pe.Else():
                            slots_t(y, 1, SURE)
                        layer1(y, 0, range(3, 6))
                    layer2(x, 3)
                    if not last:
                        layer1(y, 0, range(6, 8))
                    layer2_tail(x, count, SURE)
                if ffn == 1:
                    break

                def qkv(c, i):
                    which, m = ((0, 0), (1, 0), (0, 1), (1, 1), (2, 0), (2, 1))[i]
                    u = 6 * c + i
                    pe.wait_ge(a_zl, KD * (c + 1))
                    pe.wait_ge(s_wal, 1)
                    after(pe, a_ev, u - 2)
                    ms = slice(m * P, (m + 1) * P)
                    for k in range(KD):
                        q = three(bank[2 + u % 3][:], wah[:, k, which, ms], wal[:, k, which, ms],
                                  zh[c % 2][:, k, :], zl[c % 2][:, k, :], k == 0, k == KD - 1)
                    q.then_inc(a_qkv, 1)

                def coeff(c, m):
                    pe.wait_ge(a_el, KD * c + m + 1)
                    after(pe, a_o, KD * c + m)
                    if m == 0 and c >= 3:
                        pe.wait_ge(rt_slot, SLOT * (C + c - 2))
                    t_.matmul(bank[5][:], head_r[:], eh[:, m, :], start=True, stop=False)
                    t_.matmul(bank[5][:], head_r[:], el[:, m, :], start=False, stop=True).then_inc(a_cf, 1)

                def project(c, h):
                    pe.wait_ge(a_ol, KD * (c + 1))
                    after(pe, a_x2, 2 * c + h)
                    for i in range(2 * h, 2 * h + 2):
                        for k in range(KD):
                            ns = slice(i * P, (i + 1) * P)
                            q = three(bank[6][:, (i % 2) * D:(i % 2) * D + D], oh[:, k, ns], ol[:, k, ns],
                                      wah[:, k, 3, :], wal[:, k, 3, :], k == 0, k == KD - 1)
                    q.then_inc(a_y, 1)

                pe.wait_ge(e_w1l, KD * (Turn(1, 0, 0).g + 1))
                pe.wait_ge(s_x[0], 32)
                warm_up(WARM, 7)
                for s in range(-1, C + 4):
                    now, prev = 0 <= s < C, 0 <= s - 1 < C
                    if prev:
                        coeff(s - 1, 0)
                    if now:
                        for i in range(3):
                            qkv(s, i)
                    idle = IDLE.get(s - C, (0, 0, 0))
                    if s == C:
                        pe.wait_ge(a_ev, 6 * C)
                    warm_up(idle[0], 2)
                    if prev:
                        coeff(s - 1, 1)
                    if 0 <= s + 1 < C:
                        after(pe, r_tc, KD * (C + s - 2))
                        transpose_z(s + 1, s + 1, za, a_z, a_t)
                    if now:
                        for i in range(3, 6):
                            qkv(s, i)
                    warm_up(idle[1], 2)
                    if 0 <= s - 3 < C:
                        if prev:
                            pe.wait_ge(a_o, KD * s)
                        counts(C + s - 3)
                    if prev:
                        warm_up(idle[2], 2)
                    if prev:
                        project(s - 1, 0)
                    if 0 <= s - 2 < C:
                        after(pe, a_zl, KD * min(s + 2, C))
                        transpose_z(s - 2, C + s - 2, zr, r_z, r_t)
                    if prev:
                        project(s - 1, 1)
                    else:
                        warm_up(idle[2], 2)
                    if 0 <= s - 2 < C:
                        router_logits(C + s - 2)


_OUT = (8, 512, 256)


def kernel(L0_attn_x, L0_attn_Wq, L0_attn_bq, L0_attn_Wk, L0_attn_bk, L0_attn_Wv, L0_attn_bv, L0_attn_Wo,
           L0_attn_bo, L0_ffn_wg, L0_ffn_W1, L0_ffn_b1, L0_ffn_W2, L0_ffn_b2):
    import numpy as np
    import concourse.bacc as bacc
    from concourse.bass_utils import run_bass_kernel_spmd

    a = np.ascontiguousarray
    wa = np.stack([L0_attn_Wq, L0_attn_Wk, L0_attn_Wv, L0_attn_Wo], 1)
    w1 = np.asarray(L0_ffn_W1).reshape(E, KD, P, F).transpose(0, 2, 1, 3).reshape(E * P, KD * F)
    w2 = np.asarray(L0_ffn_W2).reshape(E, FB, P, D).transpose(0, 2, 1, 3).reshape(E * P, FB * D)
    arrays = {
        "x": a(np.asarray(L0_attn_x).reshape(T, P, D).transpose(1, 0, 2).reshape(N, D)),
        "w12": a(np.concatenate([w1, w2], 1)),
        "b1": a(np.asarray(L0_ffn_b1).reshape(E, FB, P).transpose(0, 2, 1).reshape(E * P, FB)),
        "b2": a(np.asarray(L0_ffn_b2)),
        "wa": a(wa.reshape(KD, P, 4 * D).transpose(1, 0, 2).reshape(P, KD * 4 * D)),
        "bqkv": a(np.stack([L0_attn_bq, L0_attn_bk, L0_attn_bv]).reshape(3, KD, P).transpose(2, 0, 1)),
        "bo": a(np.asarray(L0_attn_bo).reshape(1, D)),
        "wg": a(np.asarray(L0_ffn_wg).reshape(KD, P, E).transpose(1, 0, 2)),
    }
    nc = bacc.Bacc("TRN2", target_bir_lowering=False, num_devices=1)
    args = [nc.dram_tensor(n, v.shape, mybir.dt.from_np(v.dtype), kind="ExternalInput").ap()
            for n, v in arrays.items()]
    out = nc.dram_tensor("out", (N, D), F32, kind="ExternalOutput").ap()
    macaron(nc, *args, out)
    r = run_bass_kernel_spmd(nc, [arrays], core_ids=[0])
    return a(r.results[0]["out"].reshape(P, T, D).transpose(1, 0, 2)).reshape(_OUT)
```
